# Optimizing a Trainium2 kernel written in Bass

```python
import numpy as np
import jax
import jax.numpy as jnp

def _softmax(x, axis=-1):
    return jax.nn.softmax(x, axis=axis)

def _gelu(x):
    return jax.nn.gelu(x, approximate=True)

def _silu(x):
    return jax.nn.silu(x)

def _sigmoid(x):
    return jax.nn.sigmoid(x)

def _layernorm(x, axis=-1, eps=1e-05):
    m = jnp.mean(x, axis=axis, keepdims=True)
    v = jnp.var(x, axis=axis, keepdims=True)
    return (x - m) / jnp.sqrt(v + eps)

def _scatter_add(tgt, idx, src, axis=0):
    return tgt.at[idx].add(src)

def _segment_sum(src, seg, n):
    return jax.ops.segment_sum(src, seg, n)
kernel_name = 'mk_vit_tower_d1_tok_img512_r4_b5b8f3'

def setup_inputs(seed: int=0):
    np.random.seed(seed)
    _w = jnp.asarray

    def _rec_inputs():
        import jax
        import jax.numpy as jnp
        _rk = jax.random.key(seed)
        x = 7.57192e-06 + 1.00007 * jax.random.normal(jax.random.fold_in(_rk, 1), (64, 112, 112, 3), jnp.float32)
        return x
    x = _rec_inputs()

    def _L0_tok_setup():
        import jax, jax.numpy as jnp
        import numpy as np
        B, H, W, C = (64, 224, 224, 3)
        P, D = (16, 128)
        LN_EPS = 0.001

        def _shift4(x):
            pad = lambda a, spec: jnp.pad(a, spec)
            right = pad(x[:, :, :-1, :], ((0, 0), (0, 0), (1, 0), (0, 0)))
            left = pad(x[:, :, 1:, :], ((0, 0), (0, 0), (0, 1), (0, 0)))
            down = pad(x[:, :-1, :, :], ((0, 0), (1, 0), (0, 0), (0, 0)))
            up = pad(x[:, 1:, :, :], ((0, 0), (0, 1), (0, 0), (0, 0)))
            return [right, left, down, up]
        key = jax.random.key(seed)
        k0, k1, k2 = jax.random.split(key, 3)
        x = jax.random.normal(k0, (B, H, W, C), jnp.float32)
        conv_w = jax.random.normal(k1, (P, P, 5 * C, D), jnp.float32) * 0.02
        conv_b = jnp.zeros((D,), jnp.float32)
        gamma = jnp.ones((D,), jnp.float32)
        beta = jnp.zeros((D,), jnp.float32)
        dense_w = jax.random.normal(k2, (D, D), jnp.float32) * 0.02
        dense_b = jnp.zeros((D,), jnp.float32)
        return {'x': x, 'conv_w': conv_w, 'conv_b': conv_b, 'gamma': gamma, 'beta': beta, 'dense_w': dense_w, 'dense_b': dense_b}
    _L0_tok_all = _L0_tok_setup()
    _L0_tok_in = {k: v for k, v in _L0_tok_all.items() if k in ('conv_w', 'conv_b', 'gamma', 'beta', 'dense_w', 'dense_b')}
    del _L0_tok_all

    def _L0_attn_setup():
        import jax, jax.numpy as jnp
        import numpy as np
        DIM = 128
        NUM_HEADS = 8
        DIM_HEAD = 64
        EPS = 1e-08
        ROPE_THETA = 10000.0

        def rms_norm(x, gamma):
            norm = jnp.sqrt(jnp.sum(x * x, axis=-1, keepdims=True))
            x = x / jnp.maximum(norm, EPS)
            return x * DIM ** 0.5 * gamma

        def apply_rope(x):
            n, d = (x.shape[-2], x.shape[-1])
            inv_freq = 1.0 / ROPE_THETA ** (jnp.arange(0, d, 2, dtype=jnp.float32) / d)
            freqs = jnp.arange(n, dtype=jnp.float32)[:, None] * inv_freq[None, :]
            freqs = jnp.repeat(freqs, 2, axis=-1)
            cos, sin = (jnp.cos(freqs), jnp.sin(freqs))
            x1 = x[..., ::2]
            x2 = x[..., 1::2]
            rot = jnp.stack((-x2, x1), axis=-1).reshape(x.shape)
            return x * cos + rot * sin
        key = jax.random.key(seed)
        k1, k2, k3, k4 = jax.random.split(key, 4)
        b, n = (4, 512)
        dim_inner = NUM_HEADS * DIM_HEAD
        x = jax.random.normal(k1, (b, n, DIM), dtype=jnp.float32)
        gamma = jnp.ones((DIM,), dtype=jnp.float32)
        w_qkv = jax.random.normal(k2, (DIM, 3 * dim_inner), dtype=jnp.float32) * DIM ** (-0.5)
        w_out = jax.random.normal(k3, (dim_inner, DIM), dtype=jnp.float32) * dim_inner ** (-0.5)
        return {'x': x, 'gamma': gamma, 'w_qkv': w_qkv, 'w_out': w_out}
    _L0_attn_all = _L0_attn_setup()
    _L0_attn_in = {k: v for k, v in _L0_attn_all.items() if k in ('gamma', 'w_qkv', 'w_out')}
    del _L0_attn_all

    def _L0_ffn_setup():
        import jax, jax.numpy as jnp
        import numpy as np
        K = 2
        key = jax.random.key(seed)
        ks = jax.random.split(key, 6)
        B, T, d, E, dff = (2, 512, 128, 8, 512)
        x = jax.random.normal(ks[0], (B, T, d), dtype=jnp.float32)
        Wg = jax.random.normal(ks[1], (d, E), dtype=jnp.float32) * 0.02
        W1 = jax.random.normal(ks[2], (E, d, dff), dtype=jnp.float32) * 0.02
        b1 = jnp.zeros((E, dff), dtype=jnp.float32)
        W2 = jax.random.normal(ks[3], (E, dff, d), dtype=jnp.float32) * 0.02
        b2 = jnp.zeros((E, d), dtype=jnp.float32)
        return {'x': x, 'Wg': Wg, 'W1': W1, 'b1': b1, 'W2': W2, 'b2': b2}
    _L0_ffn_all = _L0_ffn_setup()
    _L0_ffn_in = {k: v for k, v in _L0_ffn_all.items() if k in ('Wg', 'W1', 'b1', 'W2', 'b2')}
    del _L0_ffn_all
    return {'x': x, 'L0_tok_conv_w': _L0_tok_in['conv_w'], 'L0_tok_conv_b': _L0_tok_in['conv_b'], 'L0_tok_gamma': _L0_tok_in['gamma'], 'L0_tok_beta': _L0_tok_in['beta'], 'L0_tok_dense_w': _L0_tok_in['dense_w'], 'L0_tok_dense_b': _L0_tok_in['dense_b'], 'L0_attn_gamma': _L0_attn_in['gamma'], 'L0_attn_w_qkv': _L0_attn_in['w_qkv'], 'L0_attn_w_out': _L0_attn_in['w_out'], 'L0_ffn_Wg': _L0_ffn_in['Wg'], 'L0_ffn_W1': _L0_ffn_in['W1'], 'L0_ffn_b1': _L0_ffn_in['b1'], 'L0_ffn_W2': _L0_ffn_in['W2'], 'L0_ffn_b2': _L0_ffn_in['b2']}

def reference(x, L0_tok_conv_w, L0_tok_conv_b, L0_tok_gamma, L0_tok_beta, L0_tok_dense_w, L0_tok_dense_b, L0_attn_gamma, L0_attn_w_qkv, L0_attn_w_out, L0_ffn_Wg, L0_ffn_W1, L0_ffn_b1, L0_ffn_W2, L0_ffn_b2):
    import jax
    import jax.numpy as jnp

    def _L0_tok_ref(x, conv_w, conv_b, gamma, beta, dense_w, dense_b):
        import jax, jax.numpy as jnp
        import numpy as np
        B, H, W, C = (64, 224, 224, 3)
        P, D = (16, 128)
        LN_EPS = 0.001

        def _shift4(x):
            pad = lambda a, spec: jnp.pad(a, spec)
            right = pad(x[:, :, :-1, :], ((0, 0), (0, 0), (1, 0), (0, 0)))
            left = pad(x[:, :, 1:, :], ((0, 0), (0, 0), (0, 1), (0, 0)))
            down = pad(x[:, :-1, :, :], ((0, 0), (1, 0), (0, 0), (0, 0)))
            up = pad(x[:, 1:, :, :], ((0, 0), (0, 1), (0, 0), (0, 0)))
            return [right, left, down, up]
        xs = jnp.concatenate([x, *_shift4(x)], axis=-1)
        y = jax.lax.conv_general_dilated(xs, conv_w, window_strides=(P, P), padding='VALID', dimension_numbers=('NHWC', 'HWIO', 'NHWC')) + conv_b
        y = y.reshape(y.shape[0], -1, D)
        mu = jnp.mean(y, axis=-1, keepdims=True)
        var = jnp.mean(jnp.square(y - mu), axis=-1, keepdims=True)
        y = (y - mu) * jax.lax.rsqrt(var + LN_EPS) * gamma + beta
        return y @ dense_w + dense_b

    def _L0_attn_ref(x, gamma, w_qkv, w_out):
        import jax, jax.numpy as jnp
        import numpy as np
        DIM = 128
        NUM_HEADS = 8
        DIM_HEAD = 64
        EPS = 1e-08
        ROPE_THETA = 10000.0

        def rms_norm(x, gamma):
            norm = jnp.sqrt(jnp.sum(x * x, axis=-1, keepdims=True))
            x = x / jnp.maximum(norm, EPS)
            return x * DIM ** 0.5 * gamma

        def apply_rope(x):
            n, d = (x.shape[-2], x.shape[-1])
            inv_freq = 1.0 / ROPE_THETA ** (jnp.arange(0, d, 2, dtype=jnp.float32) / d)
            freqs = jnp.arange(n, dtype=jnp.float32)[:, None] * inv_freq[None, :]
            freqs = jnp.repeat(freqs, 2, axis=-1)
            cos, sin = (jnp.cos(freqs), jnp.sin(freqs))
            x1 = x[..., ::2]
            x2 = x[..., 1::2]
            rot = jnp.stack((-x2, x1), axis=-1).reshape(x.shape)
            return x * cos + rot * sin
        b, n, _ = x.shape
        h, d = (NUM_HEADS, DIM_HEAD)
        xn = rms_norm(x, gamma)
        qkv = xn @ w_qkv
        qkv = qkv.reshape(b, n, 3, h, d)
        q = jnp.transpose(qkv[:, :, 0], (0, 2, 1, 3))
        k = jnp.transpose(qkv[:, :, 1], (0, 2, 1, 3))
        v = jnp.transpose(qkv[:, :, 2], (0, 2, 1, 3))
        q = apply_rope(q)
        k = apply_rope(k)
        scale = d ** (-0.5)
        attn = jnp.einsum('bhnd,bhmd->bhnm', q, k) * scale
        attn = jax.nn.softmax(attn, axis=-1)
        out = jnp.einsum('bhnm,bhmd->bhnd', attn, v)
        out = jnp.transpose(out, (0, 2, 1, 3)).reshape(b, n, h * d)
        return out @ w_out

    def _L0_ffn_ref(x, Wg, W1, b1, W2, b2):
        import jax, jax.numpy as jnp
        import numpy as np
        K = 2
        logits = jnp.einsum('btd,de->bte', x, Wg)
        probs = jax.nn.softmax(logits, axis=-1)
        top_p, _top_i = jax.lax.top_k(probs, K)
        top_p = top_p / jnp.sum(top_p, axis=-1, keepdims=True)
        b2_sum = jnp.sum(b2, axis=0)
        out = jnp.zeros_like(x)
        for i in range(K):
            w_in = x * top_p[..., i:i + 1]
            h = jax.nn.gelu(jnp.einsum('btd,edf->ebtf', w_in, W1) + b1[:, None, None, :], approximate=False)
            out = out + jnp.einsum('ebtf,efd->btd', h, W2) + b2_sum
        return out
    h = _L0_tok_ref(x, L0_tok_conv_w, L0_tok_conv_b, L0_tok_gamma, L0_tok_beta, L0_tok_dense_w, L0_tok_dense_b)
    h = h + _L0_attn_ref(_layernorm(h, axis=-1), L0_attn_gamma, L0_attn_w_qkv, L0_attn_w_out)
    h = h + _L0_ffn_ref(_layernorm(h, axis=-1), L0_ffn_Wg, L0_ffn_W1, L0_ffn_b1, L0_ffn_W2, L0_ffn_b2)
    return h

_drawn_inputs = setup_inputs


def setup_inputs(seed=0):
    import zlib

    import numpy as np

    out = dict(_drawn_inputs(seed))
    spreads = {'L0_tok_conv_b': (0.0, 0.1),
     'L0_tok_gamma': (1.0, 0.2),
     'L0_tok_beta': (0.0, 0.1),
     'L0_tok_dense_b': (0.0, 0.1),
     'L0_attn_gamma': (1.0, 0.2),
     'L0_ffn_b1': (0.0, 0.1),
     'L0_ffn_b2': (0.0, 0.1)}
    factors = {}
    for name, (base, spread) in spreads.items():
        noise = np.random.default_rng([zlib.crc32(name.encode()), seed]).standard_normal(out[name].shape)
        drawn = base * np.exp(spread * noise) if base else spread * noise
        out[name] = jnp.asarray(drawn.astype(out[name].dtype))
    for name, factor in factors.items():
        out[name] = (out[name] * factor).astype(out[name].dtype)
    return out
```

```python
from contextlib import ExitStack

import numpy as np

import concourse.bass as bass
from concourse import mybir

F32 = mybir.dt.float32
F32R = mybir.dt.float32r
F16 = mybir.dt.float16
ALU = mybir.AluOpType
ACT = mybir.ActivationFunctionType
AX_X = mybir.AxisListType.X

D = 128
N = 49
IMAGES = 64
GROUPS = 8
GI = IMAGES // GROUPS
T = GI * N
TOKENS = IMAGES * N
PATCH, SIDE, CH = 16, 7, 3
K_CONV = 960
KC = 8
KP = K_CONV // KC
PAIRS = 4
HD = 64
QT = T // 4
EXPERTS, DFF = 8, 512
FC = EXPERTS * DFF // D
TAB = 64
LOG_SCALE = 2.0 ** 20
RMS_FLOOR = (1e-8 ** 2 / D) * 1e-5

C_IDENT, C_CENTRE, C_HEADS, C_HEADROWS, C_NEGID, C_COS, C_SIN = 0, 128, 256, 384, 512, 561, 953
C_WIDTH = 953 + 392
V_CONVB, V_GAMMA, V_BETA, V_DENSEB, V_ATTNG, V_B1, V_B2 = 0, 1, 2, 3, 4, 5, 37
V_WIDTH = 45


def vit_tower(nc, patches, shifted_w, vectors, dense_w, w_qkv, w_out, w_gate, w1, w2, consts, out):
    with ExitStack() as ctx:
        def sem(name):
            return ctx.enter_context(nc.semaphore(name))

        def sb(name, shape, dt=F32, scope=ctx):
            return scope.enter_context(nc.sbuf_tensor(name, shape, dt))

        psum = ctx.enter_context(nc.psum_tensor("psum", [128, 8, 512], F32))
        const = sb("const", [128, C_WIDTH])
        vec = sb("vec", [128, V_WIDTH])
        ident = const[:, C_IDENT:C_IDENT + 128]
        centre = const[:, C_CENTRE:C_CENTRE + 128]
        ones = sb("ones", [128, 128])
        ones_mean = sb("ones_mean", [128, 128])
        cols = sb("cols", [128, 4])
        eps_conv, eps_ln, ln_shift, b2_sum = (cols[:, i:i + 1] for i in range(4))
        residual = sb("residual", [128, TOKENS])
        normed = sb("normed", [128, TOKENS])
        scales = sb("scales", [128, GROUPS, 2 * T])
        w1_hi = sb("w1_hi", [128, FC * D], F32R)
        w1_lo = sb("w1_lo", [128, FC * D], F32R)

        two = ctx.enter_context(ExitStack())
        wqk_hi = sb("wqk_hi", [128, 2, 8 * D], F32R, two)
        wqk_lo = sb("wqk_lo", [128, 2, 8 * D], F32R, two)
        wv_hi = sb("wv_hi", [128, 4 * D], F32R, two)
        wv_lo = sb("wv_lo", [128, 4 * D], F32R, two)
        wo_sb = sb("wo_sb", [128, PAIRS, D], F32, two)
        wg_sb = sb("wg_sb", [128, EXPERTS], F32, two)
        heads_r = sb("heads_r", [128, 128], F32R, two)
        headrows = sb("headrows", [128, 128], F16, two)

        with ExitStack() as own:
            shifts = sb("shifts", [KP, 5, KC * D], F32, own)
            conv_w = sb("conv_w", [KP, KC, D], F32, own)
            conv_mean = sb("conv_mean", [KP, KC], F32, own)
            patch = sb("patch", [KP, KC, T], F32, own)
            dense_raw = sb("dense_raw", [128, D], F32, own)
            dense_g = sb("dense_g", [128, D], F32, own)
            dense_c = sb("dense_c", [128, D], F32, own)
            dense_mean = sb("dense_mean", [128, 1], F32, own)
            conv_bc = sb("conv_bc", [128, 1], F32, own)
            dense_b = sb("dense_b", [128, 1], F32, own)
            dense_bc = sb("dense_bc", [128, 1], F32, own)
            qkv_raw = sb("qkv_raw", [128, 12 * D], F32, own)
            w1_raw = sb("w1_raw", [128, FC * D], F32, own)
            y = sb("y", [128, T], F32, own)
            square = sb("square", [128, T], F32, own)
            log1 = sb("log1", [128, T], F32, own)
            rstd1 = sb("rstd1", [128, T], F32, own)
            y_normed = sb("y_normed", [128, T], F32, own)
            square2 = sb("square2", [128, T], F32, own)
            floored = sb("floored", [128, T], F32, own)
            log2 = sb("log2", [128, T], F32, own)
            rstd2 = sb("rstd2", [128, T], F32, own)

            small_in = sem("small_in")
            shifts_in = sem("shifts_in")
            qkv_in = sem("qkv_in")
            attn_in = sem("attn_in")
            ffn_in = sem("ffn_in")
            patch_in = [sem(f"patch_in{c}") for c in range(KC // 2)]
            fills = sem("fills")
            wprep = sem("wprep")
            conv_ready = sem("conv_ready")
            dense_ready = sem("dense_ready")
            bias_mm = sem("bias_mm")
            bias_ready = sem("bias_ready")
            qkv_steps = sem("qkv_steps")
            w1_hi_done = sem("w1_hi_done")
            qkv_hi_done = sem("qkv_hi_done")
            swap_done = sem("swap_done")
            conv_done = sem("conv_done")
            y_out = sem("y_out")
            var1_done = sem("var1_done")
            log1_done = sem("log1_done")
            rstd1_done = sem("rstd1_done")
            y_normed_done = sem("y_normed_done")
            dense_done = sem("dense_done")
            square2_done = sem("square2_done")
            residual_done = sem("residual_done")
            var2_done = sem("var2_done")
            floored_done = sem("floored_done")
            log2_done = sem("log2_done")
            rstd2_done = sem("rstd2_done")
            normed_done = sem("normed_done")

            Y, VAR1, PLAIN, CENTRED, VAR2, BIAS = (psum[:, i, 0:T] for i in range(6))

            block = own.enter_context(nc.Block())

            @block.sync
            def _(sp):
                for s in range(5):
                    sp.dma_start(shifts[:, s, :], shifted_w[s]).then_inc(shifts_in, 16)
                sp.dma_start(const[:, :], consts).then_inc(small_in, 16)
                sp.dma_start(vec[:, :], vectors).then_inc(small_in, 16)
                sp.dma_start(dense_raw[:, :], dense_w).then_inc(small_in, 16)
                for c in range(KC // 2):
                    sp.dma_start(patch[:, 2 * c:2 * c + 2, :], patches[0, :, 2 * c:2 * c + 2, :]).then_inc(patch_in[c], 16)
                sp.dma_start(qkv_raw[:, :], w_qkv).then_inc(qkv_in, 16)
                with sp.Fori(1, GROUPS) as g:
                    for c in range(KC // 2):
                        sp.wait_ge(conv_done, (g - 1) * (KC // 2) + c + 1)
                        sp.dma_start(patch[:, 2 * c:2 * c + 2, :],
                                     patches[bass.ds(g, 1), :, 2 * c:2 * c + 2, :].rearrange("a p c t -> p (a c) t")).then_inc(patch_in[c], 16)

            @block.scalar
            def _(act):
                act.preload_act_table_set("natural_log_exp_and_others")
                act.dma_start(w1_raw[:, :], w1).then_inc(ffn_in, 16)
                act.dma_start(wo_sb[:, :, :], w_out).then_inc(attn_in, 16)
                act.dma_start(wg_sb[:, :], w_gate).then_inc(attn_in, 16)

                def leave_conv(g):
                    act.wait_ge(conv_done, (g + 1) * (KC // 2))
                    if not (isinstance(g, int) and g == 0):
                        act.wait_ge(var1_done, g)
                    nc.scalar.activation(square[:, :], Y, ACT.Square, bias=conv_bc[:, 0:1]).then_inc(y_out, 1)
                    if not (isinstance(g, int) and g == 0):
                        act.wait_ge(y_normed_done, g)
                    nc.scalar.activation(y[:, :], Y, ACT.Identity, bias=conv_bc[:, 0:1]).then_inc(y_out, 1)

                def norm1(g):
                    act.wait_ge(var1_done, g + 1)
                    nc.scalar.activation(log1[:, :], VAR1, ACT.Ln, bias=eps_conv).then_inc(log1_done, 1)
                    act.wait_ge(log1_done, g + 1)
                    nc.scalar.activation(rstd1[:, :], log1[:, :], ACT.Exp, scale=-0.5).then_inc(rstd1_done, 1)

                def leave_dense(g):
                    act.wait_ge(dense_done, 2 * g + 1)
                    nc.scalar.activation(square2[:, :], CENTRED, ACT.Square, bias=dense_bc[:, 0:1]).then_inc(square2_done, 1)
                    act.wait_ge(dense_done, 2 * g + 2)
                    nc.scalar.activation(residual[:, bass.ds(g * T, T)], PLAIN, ACT.Identity, bias=dense_b[:, 0:1]).then_inc(residual_done, 1)

                def norm2(g):
                    act.wait_ge(floored_done, g + 1)
                    nc.scalar.activation(log2[:, :], floored[:, :], ACT.Ln, scale=LOG_SCALE).then_inc(log2_done, 1)
                    act.wait_ge(log2_done, g + 1)
                    if not (isinstance(g, int) and g == 0):
                        act.wait_ge(normed_done, g)
                    nc.scalar.activation(rstd2[:, :], log2[:, :], ACT.Exp, scale=-0.5, bias=ln_shift).then_inc(rstd2_done, 1)

                act.wait_ge(bias_ready, 3)
                leave_conv(0)
                norm1(0)
                act.wait_ge(qkv_steps, 1)
                nc.scalar.activation(wqk_hi[:, 0, :], qkv_raw[:, 0:8 * D], ACT.Copy).then_inc(qkv_hi_done, 1)
                nc.scalar.activation(wv_hi[:, :], qkv_raw[:, 8 * D:12 * D], ACT.Copy).then_inc(qkv_hi_done, 1)
                with act.Fori(1, GROUPS) as g:
                    leave_dense(g - 1)
                    leave_conv(g)
                    norm2(g - 1)
                    norm1(g)
                leave_dense(GROUPS - 1)
                norm2(GROUPS - 1)
                act.wait_ge(ffn_in, 16)
                nc.scalar.activation(w1_hi[:, :], w1_raw[:, :], ACT.Copy).then_inc(w1_hi_done, 1)

            @block.vector
            def _(dve):
                nc.vector.memset(ones[:, :], 1.0).then_inc(fills, 1)
                nc.vector.memset(ones_mean[:, :], 1.0 / D).then_inc(fills, 1)
                nc.vector.memset(eps_conv, 1e-3).then_inc(fills, 1)
                nc.vector.memset(eps_ln, 1e-5).then_inc(fills, 1)
                nc.vector.memset(ln_shift, 0.5 * float(np.log(LOG_SCALE))).then_inc(fills, 1)
                dve.wait_ge(shifts_in, 80)
                flat = conv_w[:, :, :].rearrange("p c d -> p (c d)")
                nc.vector.tensor_tensor(flat, shifts[:, 0, :], shifts[:, 1, :], ALU.add).then_inc(wprep, 1)
                for s in range(2, 5):
                    dve.wait_ge(wprep, s - 1)
                    nc.vector.tensor_tensor(flat, flat, shifts[:, s, :], ALU.add).then_inc(wprep, 1)
                dve.wait_ge(wprep, 4)
                nc.vector.tensor_reduce(conv_mean[:, :], conv_w[:, :, :], AX_X, ALU.add).then_inc(wprep, 1)
                dve.wait_ge(wprep, 5)
                nc.vector.tensor_scalar(conv_mean[:, :], conv_mean[:, :], 1.0 / D, None, ALU.mult).then_inc(wprep, 1)
                dve.wait_ge(wprep, 6)
                nc.vector.tensor_tensor(conv_w[:, :, :], conv_w[:, :, :],
                                        conv_mean[:, :].unsqueeze(2).broadcast_to([KP, KC, D]), ALU.subtract).then_inc(conv_ready, 1)
                dve.wait_ge(small_in, 48)
                nc.vector.tensor_scalar(dense_g[:, :], dense_raw[:, :], vec[:, V_GAMMA:V_GAMMA + 1], None, ALU.mult).then_inc(wprep, 1)
                dve.wait_ge(wprep, 7)
                nc.vector.tensor_reduce(dense_mean[:, :], dense_g[:, :], AX_X, ALU.add).then_inc(wprep, 1)
                dve.wait_ge(wprep, 8)
                nc.vector.tensor_scalar(dense_mean[:, :], dense_mean[:, :], 1.0 / D, None, ALU.mult).then_inc(wprep, 1)
                dve.wait_ge(wprep, 9)
                nc.vector.tensor_scalar(dense_c[:, :], dense_g[:, :], dense_mean[:, 0:1], None, ALU.subtract).then_inc(dense_ready, 1)
                dve.wait_ge(bias_mm, 1)
                nc.vector.tensor_copy(conv_bc[:, :], BIAS[:, 0:1]).then_inc(bias_ready, 1)
                nc.vector.tensor_tensor(dense_b[:, :], BIAS[:, 1:2], vec[:, V_DENSEB:V_DENSEB + 1], ALU.add).then_inc(bias_ready, 1)
                dve.wait_ge(bias_mm, 2)
                nc.vector.tensor_copy(dense_bc[:, :], BIAS[:, 2:3]).then_inc(bias_ready, 1)
                nc.vector.tensor_copy(headrows[:, :], const[:, C_HEADROWS:C_HEADROWS + 128]).then_inc(wprep, 1)
                nc.vector.tensor_copy(heads_r[:, :], const[:, C_HEADS:C_HEADS + 128]).then_inc(wprep, 1)
                nc.vector.tensor_reduce(b2_sum, vec[:, V_B2:V_B2 + EXPERTS], AX_X, ALU.add).then_inc(wprep, 1)
                dve.wait_ge(wprep, 12)
                nc.vector.tensor_scalar(b2_sum, b2_sum, 2.0, None, ALU.mult).then_inc(wprep, 1)

                def scale1(g):
                    dve.wait_ge(rstd1_done, g + 1)
                    dve.wait_ge(y_out, 2 * g + 2)
                    if not (isinstance(g, int) and g == 0):
                        dve.wait_ge(dense_done, 2 * g)
                    nc.vector.tensor_tensor(y_normed[:, :], y[:, :], rstd1[:, :], ALU.mult).then_inc(y_normed_done, 1)

                def scale2(g):
                    dve.wait_ge(var2_done, g + 1)
                    if not (isinstance(g, int) and g == 0):
                        dve.wait_ge(log2_done, g)
                    nc.vector.tensor_scalar(floored[:, :], VAR2, RMS_FLOOR, None, ALU.max).then_inc(floored_done, 1)
                    dve.wait_ge(rstd2_done, g + 1)
                    nc.vector.scalar_tensor_tensor(out=normed[:, bass.ds(g * T, T)], in0=CENTRED, scalar=dense_bc[:, 0:1],
                                                   in1=rstd2[:, :], op0=ALU.add, op1=ALU.mult).then_inc(normed_done, 1)

                scale1(0)
                for part, src in enumerate((wqk_hi, wqk_lo)):
                    if part == 0:
                        dve.wait_ge(qkv_hi_done, 2)
                    else:
                        dve.wait_ge(qkv_steps, 3)
                    pairs = src[:, :, :].bitcast(F32).rearrange("p s (c e) -> p s c e", e=2)
                    outs = src[:, :, :].rearrange("p s (c e) -> p s c e", e=2)
                    nc.vector.tensor_copy(outs[:, 1, :, 0], pairs[:, 0, :, 1]).then_inc(swap_done, 1)
                    nc.vector.tensor_copy(outs[:, 1, :, 1], pairs[:, 0, :, 0]).then_inc(swap_done, 1)
                with dve.Fori(1, GROUPS) as g:
                    scale2(g - 1)
                    scale1(g)
                scale2(GROUPS - 1)

            @block.gpsimd
            def _(pool):
                pool.wait_ge(qkv_in, 16)
                pool.wait_ge(small_in, 48)
                nc.gpsimd.tensor_scalar(qkv_raw[:, :], qkv_raw[:, :], vec[:, V_ATTNG:V_ATTNG + 1], None, ALU.mult).then_inc(qkv_steps, 1)
                pool.wait_ge(qkv_hi_done, 2)
                nc.gpsimd.tensor_tensor(wv_lo[:, :], qkv_raw[:, 8 * D:12 * D], wv_hi[:, :].bitcast(F32), ALU.subtract).then_inc(qkv_steps, 1)
                nc.gpsimd.tensor_tensor(wqk_lo[:, 0, :], qkv_raw[:, 0:8 * D], wqk_hi[:, 0, :].bitcast(F32), ALU.subtract).then_inc(qkv_steps, 1)
                pool.wait_ge(w1_hi_done, 1)
                nc.gpsimd.tensor_tensor(w1_lo[:, :], w1_raw[:, :], w1_hi[:, :].bitcast(F32), ALU.subtract).then_inc(qkv_steps, 1)

            @block.tensor
            def _(pe):
                def conv(g, first, last):
                    if first == 0 and not (isinstance(g, int) and g == 0):
                        pe.wait_ge(y_out, 2 * g)
                    for c in range(first, last):
                        if c % 2 == 0:
                            pe.wait_ge(patch_in[c // 2], 16 * g + 16)
                        mm = pe.matmul(Y, conv_w[:, c, :], patch[:, c, :], start=(c == 0), stop=(c == KC - 1))
                        if c % 2:
                            mm.then_inc(conv_done, 1)

                def variance1(g):
                    pe.wait_ge(y_out, 2 * g + 1)
                    if not (isinstance(g, int) and g == 0):
                        pe.wait_ge(log1_done, g)
                    pe.matmul(VAR1, ones_mean[:, :], square[:, :], start=True, stop=True).then_inc(var1_done, 1)

                def dense(g):
                    pe.wait_ge(y_normed_done, g + 1)
                    if not (isinstance(g, int) and g == 0):
                        pe.wait_ge(normed_done, g)
                    pe.matmul(CENTRED, dense_c[:, :], y_normed[:, :], start=True, stop=True).then_inc(dense_done, 1)
                    if not (isinstance(g, int) and g == 0):
                        pe.wait_ge(residual_done, g)
                    pe.matmul(PLAIN, dense_g[:, :], y_normed[:, :], start=True, stop=True).then_inc(dense_done, 1)

                def variance2(g):
                    pe.wait_ge(square2_done, g + 1)
                    if not (isinstance(g, int) and g == 0):
                        pe.wait_ge(floored_done, g)
                    pe.matmul(VAR2, ones_mean[:, :], square2[:, :], start=True, stop=True).then_inc(var2_done, 1)

                pe.wait_ge(dense_ready, 1)
                pe.matmul(BIAS[:, 0:1], centre, vec[:, V_CONVB:V_CONVB + 1], start=True, stop=True)
                pe.matmul(BIAS[:, 1:2], dense_raw[:, :], vec[:, V_BETA:V_BETA + 1], start=True, stop=True).then_inc(bias_mm, 1)
                pe.wait_ge(bias_ready, 2)
                pe.matmul(BIAS[:, 2:3], centre, dense_b[:, :], start=True, stop=True).then_inc(bias_mm, 1)
                pe.wait_ge(conv_ready, 1)
                pe.wait_ge(fills, 5)
                conv(0, 0, KC)
                with pe.Fori(1, GROUPS) as g:
                    conv(g, 0, 3)
                    variance1(g - 1)
                    conv(g, 3, 6)
                    dense(g - 1)
                    conv(g, 6, KC)
                    variance2(g - 1)
                variance1(GROUPS - 1)
                dense(GROUPS - 1)
                variance2(GROUPS - 1)

        with ExitStack() as own:
            x_hi = sb("x_hi", [128, T], F32R, own)
            x_lo = sb("x_lo", [128, T], F32R, own)
            xv_hi = sb("xv_hi", [128, GI, TAB], F32R, own)
            xv_lo = sb("xv_lo", [128, GI, TAB], F32R, own)
            term = sb("term", [128, 4, T], F32, own)
            q_sum = sb("q_sum", [128, 2, T], F32, own)
            k_sum = sb("k_sum", [128, 2, T], F32, own)
            q_hi = sb("q_hi", [128, PAIRS, T], F16, own)
            q_lo = sb("q_lo", [128, PAIRS, T], F16, own)
            k_hi = sb("k_hi", [128, PAIRS, GI, 2 * TAB], F16, own)
            k_lo = sb("k_lo", [128, PAIRS, GI, 2 * TAB], F16, own)
            v_hi = sb("v_hi", [128, GI, PAIRS, D], F16, own)
            v_lo = sb("v_lo", [128, GI, PAIRS, D], F16, own)
            row_max = sb("row_max", [128, 2, GI], F32, own)
            neg_max = sb("neg_max", [128, 2, T], F32R, own)
            prob = sb("prob", [128, 2, T], F32, own)
            prob_hi = sb("prob_hi", [128, 2, T], F16, own)
            prob_lo = sb("prob_lo", [128, 2, T], F16, own)
            inv_den = sb("inv_den", [128, 2, T], F32, own)
            heads_out = sb("heads_out", [128, PAIRS, T], F32, own)
            square3 = sb("square3", [128, T], F32, own)
            rstd3 = sb("rstd3", [128, T], F32, own)
            ffn_x = sb("ffn_x", [128, T], F32, own)
            top = sb("top", [QT, 4, 8], F32, own)
            gap = sb("gap", [QT, 4], F32, own)
            ratio = sb("ratio", [QT, 4], F32, own)
            den2 = sb("den2", [QT, 4], F32, own)
            weight = sb("weight", [QT, 2, 4], F32, own)
            weight_diag = sb("weight_diag", [QT, 8, QT], F32, own)

            s_fill = sem("s_fill")
            s_fill_dve = sem("s_fill_dve")
            x_hi_done = sem("x_hi_done")
            x_lo_done = sem("x_lo_done")
            xv_done = sem("xv_done")
            proj_done = sem("proj_done")
            proj_left = sem("proj_left")
            rope_done = sem("rope_done")
            qk_hi_done = sem("qk_hi_done")
            qk_lo_done = sem("qk_lo_done")
            v_hi_done = sem("v_hi_done")
            scores_done = sem("scores_done")
            max_done = sem("max_done")
            neg_done = sem("neg_done")
            logits_done = sem("logits_done")
            prob_done = sem("prob_done")
            prob_lo_done = sem("prob_lo_done")
            den_done = sem("den_done")
            pv_done = sem("pv_done")
            log_den_done = sem("log_den_done")
            inv_done = sem("inv_done")
            heads_done = sem("heads_done")
            attn_done = sem("attn_done")
            h1_done = sem("h1_done")
            centre_done = sem("centre_done")
            square3_done = sem("square3_done")
            var3_done = sem("var3_done")
            log3_done = sem("log3_done")
            rstd3_done = sem("rstd3_done")
            ffn_x_done = sem("ffn_x_done")
            router_done = sem("router_done")
            top_done = sem("top_done")
            small_done = sem("small_done")
            ratio_done = sem("ratio_done")
            diag_done = sem("diag_done")
            spread_done = sem("spread_done")
            scales_done = sem("scales_done")
            ffn_in_done = sem("ffn_in_done")

            P0, P1, SC, LG, OUT, DEN, X0, X1 = range(8)
            cos = const[:, C_COS:C_COS + T]
            sin = const[:, C_SIN:C_SIN + T]
            neg_id = const[:, C_NEGID:C_NEGID + N].unsqueeze(1).broadcast_to([128, GI, N])
            ITEMS = 20
            FIRST = (0, 8, 12, 16)
            V_FIRST = 4

            block = own.enter_context(nc.Block())

            def zero(g):
                return isinstance(g, int) and g == 0

            @block.tensor
            def _(pe):
                def bank(i):
                    return psum[:, P0 + i % 2, :]

                def claim(g, i):
                    if not (zero(g) and i < 2):
                        pe.wait_ge(proj_left, ITEMS * g + i - 1)

                def project(g, j):
                    if j == 0:
                        pe.wait_ge(x_lo_done, g + 1)
                    for n, (side, swapped) in enumerate(((0, 0), (0, 1), (1, 0), (1, 1))):
                        i = FIRST[j] + n
                        claim(g, i)
                        at = (side * PAIRS + j) * D
                        hi, lo = wqk_hi[:, swapped, at:at + D], wqk_lo[:, swapped, at:at + D]
                        to = bank(i)[:, 0:T]
                        pe.matmul(to, hi, x_hi[:, 0:T], start=True, stop=False)
                        pe.matmul(to, hi, x_lo[:, 0:T], start=False, stop=False)
                        pe.matmul(to, lo, x_hi[:, 0:T], start=False, stop=True).then_inc(proj_done, 1)

                def values(g):
                    pe.wait_ge(xv_done, 2 * g + 2)
                    for p in range(GI // 2):
                        i = V_FIRST + p
                        claim(g, i)
                        hi = xv_hi[:, 2 * p:2 * p + 2, :].rearrange("p b n -> p (b n)")
                        lo = xv_lo[:, 2 * p:2 * p + 2, :].rearrange("p b n -> p (b n)")
                        to = bank(i)
                        pe.matmul(to, hi, wv_hi[:, :], start=True, stop=False)
                        pe.matmul(to, lo, wv_hi[:, :], start=False, stop=False)
                        pe.matmul(to, hi, wv_lo[:, :], start=False, stop=True).then_inc(proj_done, 1)

                def scores(g, j):
                    pe.wait_ge(qk_hi_done, 3 * (PAIRS * g + j) + 3)
                    if not (zero(g) and j == 0):
                        pe.wait_ge(max_done, PAIRS * g + j)
                    pe.ldweights(headrows[:, :], tile_position=(0, 0))
                    for h in range(2):
                        rows = slice(TAB * h, TAB * h + TAB)
                        for b in range(GI):
                            mm = pe.matmul(psum[TAB * h:TAB * h + N, SC, b * N:b * N + N],
                                           q_hi[rows, j, b * N:b * N + N],
                                           k_hi[rows, j, b, TAB * h:TAB * h + N], start=True, stop=True)
                    mm.then_inc(scores_done, 1)

                def logits(g, j):
                    pe.wait_ge(neg_done, PAIRS * g + j + 1)
                    pe.wait_ge(qk_lo_done, 3 * (PAIRS * g + j) + 3)
                    if not (zero(g) and j == 0):
                        pe.wait_ge(prob_done, 2 * (PAIRS * g + j))
                    pe.matmul(psum[:, LG, 0:T], heads_r[:, :], neg_max[:, j % 2, :], start=True, stop=False)
                    for b in range(GI):
                        to = psum[:, LG, b * N:b * N + N]
                        qs = slice(b * N, b * N + N)
                        pe.matmul(to, k_hi[:, j, b, :], q_hi[:, j, qs], start=False, stop=False)
                        pe.matmul(to, k_hi[:, j, b, :], q_lo[:, j, qs], start=False, stop=False)
                        mm = pe.matmul(to, k_lo[:, j, b, :], q_hi[:, j, qs], start=False, stop=(b == GI - 1))
                    mm.then_inc(logits_done, 1)

                def weigh(g, j):
                    n = PAIRS * g + j
                    pe.wait_ge(prob_lo_done, n + 1)
                    if not (zero(g) and j == 0):
                        pe.wait_ge(log_den_done, n)
                    pe.matmul(psum[:, DEN, 0:T], headrows[:, :], prob_hi[:, j % 2, :], start=True, stop=False)
                    pe.matmul(psum[:, DEN, 0:T], headrows[:, :], prob_lo[:, j % 2, :], start=False, stop=True).then_inc(den_done, 1)
                    if j == 0:
                        pe.wait_ge(proj_left, ITEMS * g + V_FIRST + GI // 2)
                    if not (zero(g) and j == 0):
                        pe.wait_ge(heads_done, n)
                    for b in range(GI):
                        to = psum[:, OUT, b * N:b * N + N]
                        ps = slice(b * N, b * N + N)
                        pe.matmul(to, v_hi[:, b, j, :], prob_hi[:, j % 2, ps], start=True, stop=False)
                        pe.matmul(to, v_hi[:, b, j, :], prob_lo[:, j % 2, ps], start=False, stop=False)
                        mm = pe.matmul(to, v_lo[:, b, j, :], prob_hi[:, j % 2, ps], start=False, stop=True)
                    mm.then_inc(pv_done, 1)

                def project_out(g):
                    pe.wait_ge(heads_done, PAIRS * (g + 1))
                    if not zero(g):
                        pe.wait_ge(scales_done, 2 * g)
                    for j in range(PAIRS):
                        mm = pe.matmul(psum[:, X0, 0:T], wo_sb[:, j, :], heads_out[:, j, :], start=(j == 0), stop=(j == PAIRS - 1))
                    mm.then_inc(attn_done, 1)

                def centre_h(g):
                    pe.wait_ge(h1_done, g + 1)
                    pe.matmul(psum[:, X1, 0:T], centre, residual[:, bass.ds(g * T, T)], start=True, stop=True).then_inc(centre_done, 1)

                def variance3(g):
                    pe.wait_ge(square3_done, g + 1)
                    pe.matmul(psum[:, X0, 0:T], ones_mean[:, :], square3[:, :], start=True, stop=True).then_inc(var3_done, 1)

                def router(g):
                    pe.wait_ge(ffn_x_done, g + 1)
                    for t in range(4):
                        mm = pe.matmul(psum[0:QT, X0, 8 * t:8 * t + 8], ffn_x[:, t * QT:t * QT + QT], wg_sb[:, :], start=True, stop=True)
                    mm.then_inc(router_done, 1)

                def spread(g):
                    pe.wait_ge(diag_done, g + 1)
                    pe.matmul(psum[:, X1, 0:T], ones[0:QT, :], weight_diag[:, 0:4, :], start=True, stop=True).then_inc(spread_done, 1)
                    pe.matmul(psum[:, X0, 0:T], ones[0:QT, :], weight_diag[:, 4:8, :], start=True, stop=True).then_inc(spread_done, 1)

                def group(g, prev):
                    project(g, 0)
                    if prev is not None:
                        weigh(prev, 2)
                        weigh(prev, 3)
                    values(g)
                    project(g, 1)
                    if prev is not None:
                        project_out(prev)
                    project(g, 2)
                    if prev is not None:
                        centre_h(prev)
                    scores(g, 0)
                    project(g, 3)
                    if prev is not None:
                        variance3(prev)
                    scores(g, 1)
                    logits(g, 0)
                    if prev is not None:
                        router(prev)
                    scores(g, 2)
                    logits(g, 1)
                    weigh(g, 0)
                    if prev is not None:
                        spread(prev)
                    scores(g, 3)
                    logits(g, 2)
                    weigh(g, 1)
                    logits(g, 3)

                pe.wait_ge(s_fill, 4)
                pe.wait_ge(s_fill_dve, 3)
                pe.wait_ge(attn_in, 32)
                group(0, None)
                with pe.Fori(1, GROUPS) as g:
                    group(g, g - 1)
                last = GROUPS - 1
                weigh(last, 2)
                weigh(last, 3)
                project_out(last)
                centre_h(last)
                variance3(last)
                router(last)
                spread(last)

            @block.scalar
            def _(act):
                def high(g, j):
                    n = PAIRS * g + j
                    act.wait_ge(rope_done, 2 * n + 1)
                    if not zero(g):
                        act.wait_ge(logits_done, n - PAIRS + 1)
                    nc.scalar.activation(q_hi[:, j, :], q_sum[:, j % 2, :], ACT.Copy).then_inc(qk_hi_done, 1)
                    act.wait_ge(rope_done, 2 * n + 2)
                    for h in range(2):
                        rows = slice(TAB * h, TAB * h + TAB)
                        nc.scalar.activation(k_hi[rows, j, :, TAB * h:TAB * h + N],
                                             k_sum[rows, j % 2, :].rearrange("p (b n) -> p b n", b=GI), ACT.Copy).then_inc(qk_hi_done, 1)

                def high_values(g):
                    if not zero(g):
                        act.wait_ge(pv_done, PAIRS * g)
                    for p in range(GI // 2):
                        i = V_FIRST + p
                        act.wait_ge(proj_done, ITEMS * g + i + 1)
                        for b in range(2):
                            for h in range(2):
                                src = psum[TAB * b:TAB * b + N, P0 + i % 2, :].rearrange("p (j h d) -> p j h d", j=PAIRS, h=2)
                                nc.scalar.activation(v_hi[TAB * h:TAB * h + N, 2 * p + b, :, HD * h:HD * h + HD],
                                                     src[:, :, h, :], ACT.Copy).then_inc(v_hi_done, 1)

                def exponent(g, j):
                    n = PAIRS * g + j
                    act.wait_ge(logits_done, n + 1)
                    if not (zero(g) and j < 2):
                        act.wait_ge(den_done, n - 1)
                        act.wait_ge(pv_done, n - 1)
                    nc.scalar.activation(prob[:, j % 2, :], psum[:, LG, 0:T], ACT.Exp, scale=HD ** -0.5).then_inc(prob_done, 1)
                    nc.scalar.activation(prob_hi[:, j % 2, :], psum[:, LG, 0:T], ACT.Exp, scale=HD ** -0.5).then_inc(prob_done, 1)

                def inverse(g, j):
                    n = PAIRS * g + j
                    act.wait_ge(den_done, n + 1)
                    if not (zero(g) and j < 2):
                        act.wait_ge(heads_done, n - 1)
                    nc.scalar.activation(inv_den[:, j % 2, :], psum[:, DEN, 0:T], ACT.Ln).then_inc(log_den_done, 1)
                    act.wait_ge(log_den_done, n + 1)
                    nc.scalar.activation(inv_den[:, j % 2, :], inv_den[:, j % 2, :], ACT.Exp, scale=-1.0).then_inc(inv_done, 1)

                def square_h(g):
                    act.wait_ge(centre_done, g + 1)
                    nc.scalar.activation(square3[:, :], psum[:, X1, 0:T], ACT.Square).then_inc(square3_done, 1)

                def norm3(g):
                    act.wait_ge(var3_done, g + 1)
                    if not zero(g):
                        act.wait_ge(ffn_x_done, g)
                    nc.scalar.activation(rstd3[:, :], psum[:, X0, 0:T], ACT.Ln, bias=eps_ln).then_inc(log3_done, 1)
                    act.wait_ge(log3_done, g + 1)
                    nc.scalar.activation(rstd3[:, :], rstd3[:, :], ACT.Exp, scale=-0.5).then_inc(rstd3_done, 1)

                def router_ratio(g):
                    act.wait_ge(small_done, 4 * g + 1)
                    nc.scalar.activation(ratio[:, :], gap[:, :], ACT.Exp).then_inc(ratio_done, 1)

                def keep_scales(g):
                    for i, x in enumerate((X1, X0)):
                        act.wait_ge(spread_done, 2 * g + i + 1)
                        nc.scalar.activation(scales[:, bass.ds(g, 1), i * T:i * T + T], psum[:, x, 0:T].unsqueeze(1), ACT.Copy).then_inc(scales_done, 1)

                def group(g, prev):
                    high(g, 0)
                    if prev is not None:
                        inverse(prev, 2)
                        inverse(prev, 3)
                    high_values(g)
                    high(g, 1)
                    high(g, 2)
                    if prev is not None:
                        square_h(prev)
                    high(g, 3)
                    if prev is not None:
                        norm3(prev)
                    exponent(g, 0)
                    if prev is not None:
                        router_ratio(prev)
                    exponent(g, 1)
                    inverse(g, 0)
                    if prev is not None:
                        keep_scales(prev)
                    exponent(g, 2)
                    inverse(g, 1)
                    exponent(g, 3)

                act.preload_act_table_set("natural_log_exp_and_others")
                act.wait_ge(s_fill, 4)
                group(0, None)
                with act.Fori(1, GROUPS) as g:
                    group(g, g - 1)
                last = GROUPS - 1
                inverse(last, 2)
                inverse(last, 3)
                square_h(last)
                norm3(last)
                router_ratio(last)
                keep_scales(last)

            @block.vector
            def _(dve):
                def split(g):
                    if not zero(g):
                        dve.wait_ge(proj_done, ITEMS * g)
                    here = normed[:, bass.ds(g * T, T)]
                    nc.vector.tensor_copy(x_hi[:, 0:T], here).then_inc(x_hi_done, 1)
                    dve.wait_ge(x_hi_done, g + 1)
                    nc.vector.tensor_tensor(x_lo[:, 0:T], here, x_hi[:, 0:T].bitcast(F32), ALU.subtract).then_inc(x_lo_done, 1)
                    dve.wait_ge(x_lo_done, g + 1)
                    for to, part in ((xv_hi, x_hi), (xv_lo, x_lo)):
                        nc.vector.tensor_copy(to[:, :, 0:N], part[:, :].bitcast(F32).rearrange("p (b n) -> p b n", b=GI)).then_inc(xv_done, 1)

                def rope(g, j):
                    for n, table in enumerate((cos, sin, cos, sin)):
                        i = FIRST[j] + n
                        dve.wait_ge(proj_done, ITEMS * g + i + 1)
                        if not (zero(g) and j == 0):
                            dve.wait_ge(rope_done, 2 * (PAIRS * g + j) - 1 + n // 2)
                        nc.vector.tensor_tensor(term[:, n, :], psum[:, P0 + i % 2, 0:T], table, ALU.mult).then_inc(proj_left, 1)

                def low_values(g):
                    for p in range(GI // 2):
                        i = V_FIRST + p
                        dve.wait_ge(v_hi_done, 16 * g + 4 * p + 4)
                        for b in range(2):
                            for h in range(2):
                                src = psum[TAB * b:TAB * b + N, P0 + i % 2, :].rearrange("p (j h d) -> p j h d", j=PAIRS, h=2)
                                where = (slice(TAB * h, TAB * h + N), 2 * p + b, slice(None), slice(HD * h, HD * h + HD))
                                last = nc.vector.tensor_tensor(v_lo[where], src[:, :, h, :], v_hi[where], ALU.subtract)
                        last.then_inc(proj_left, 1)

                def row_maximum(g, j):
                    n = PAIRS * g + j
                    dve.wait_ge(scores_done, n + 1)
                    if not (zero(g) and j < 2):
                        dve.wait_ge(neg_done, n - 1)
                    nc.vector.tensor_reduce(row_max[:, j % 2, :], psum[:, SC, 0:T].rearrange("p (b n) -> p b n", b=GI),
                                            AX_X, ALU.max).then_inc(max_done, 1)

                def low_prob(g, j):
                    n = PAIRS * g + j
                    dve.wait_ge(prob_done, 2 * n + 2)
                    if not (zero(g) and j < 2):
                        dve.wait_ge(pv_done, n - 1)
                    nc.vector.tensor_tensor(prob_lo[:, j % 2, :], prob[:, j % 2, :], prob_hi[:, j % 2, :], ALU.subtract).then_inc(prob_lo_done, 1)

                def normalise(g, j):
                    n = PAIRS * g + j
                    dve.wait_ge(inv_done, n + 1)
                    dve.wait_ge(pv_done, n + 1)
                    if j == 0 and not zero(g):
                        dve.wait_ge(attn_done, g)
                    nc.vector.tensor_tensor(heads_out[:, j, :], psum[:, OUT, 0:T], inv_den[:, j % 2, :], ALU.mult).then_inc(heads_done, 1)

                def add_residual(g):
                    dve.wait_ge(attn_done, g + 1)
                    here = residual[:, bass.ds(g * T, T)]
                    nc.vector.tensor_tensor(here, psum[:, X0, 0:T], here, ALU.add).then_inc(h1_done, 1)

                def norm_ffn(g):
                    dve.wait_ge(rstd3_done, g + 1)
                    nc.vector.tensor_tensor(ffn_x[:, :], psum[:, X1, 0:T], rstd3[:, :], ALU.mult).then_inc(ffn_x_done, 1)

                def router_top(g):
                    dve.wait_ge(router_done, g + 1)
                    nc.vector.tensor_copy(normed[:, bass.ds(g * T, T)], ffn_x[:, :]).then_inc(ffn_in_done, 1)
                    for t in range(4):
                        last = nc.vector.max(out=top[:, t, :], in_=psum[0:QT, X0, 8 * t:8 * t + 8])
                    last.then_inc(top_done, 1)
                    dve.wait_ge(top_done, g + 1)
                    nc.vector.tensor_tensor(gap[:, :], top[:, :, 1], top[:, :, 0], ALU.subtract).then_inc(small_done, 1)

                def router_weights(g):
                    dve.wait_ge(ratio_done, g + 1)
                    nc.vector.tensor_scalar(den2[:, :], ratio[:, :], 1.0, None, ALU.add).then_inc(small_done, 1)
                    dve.wait_ge(small_done, 4 * g + 2)
                    nc.vector.reciprocal(weight[:, 0, :], den2[:, :]).then_inc(small_done, 1)
                    dve.wait_ge(small_done, 4 * g + 3)
                    nc.vector.tensor_tensor(weight[:, 1, :], weight[:, 0, :], ratio[:, :], ALU.mult).then_inc(small_done, 1)
                    dve.wait_ge(small_done, 4 * g + 4)
                    nc.vector.tensor_tensor(weight_diag[:, :, :],
                                            weight[:, :, :].rearrange("p i t -> p (i t)").unsqueeze(2).broadcast_to([QT, 8, QT]),
                                            ident[0:QT, 0:QT].unsqueeze(1).broadcast_to([QT, 8, QT]), ALU.mult).then_inc(diag_done, 1)

                def group(g, prev, nxt):
                    rope(g, 0)
                    if prev is not None:
                        normalise(prev, 2)
                        normalise(prev, 3)
                    low_values(g)
                    rope(g, 1)
                    if prev is not None:
                        add_residual(prev)
                    rope(g, 2)
                    row_maximum(g, 0)
                    rope(g, 3)
                    if nxt:
                        split(g + 1)
                    row_maximum(g, 1)
                    if prev is not None:
                        norm_ffn(prev)
                    low_prob(g, 0)
                    if prev is not None:
                        router_top(prev)
                    row_maximum(g, 2)
                    low_prob(g, 1)
                    normalise(g, 0)
                    if prev is not None:
                        router_weights(prev)
                    row_maximum(g, 3)
                    low_prob(g, 2)
                    normalise(g, 1)
                    low_prob(g, 3)

                nc.vector.memset(psum[:, SC, 0:T], 0.0).then_inc(s_fill_dve, 1)
                nc.vector.memset(xv_hi[:, :, :].bitcast(F32), 0.0).then_inc(s_fill_dve, 1)
                nc.vector.memset(xv_lo[:, :, :].bitcast(F32), 0.0).then_inc(s_fill_dve, 1)
                dve.wait_ge(s_fill_dve, 3)
                split(0)
                dve.wait_ge(s_fill, 4)
                group(0, None, True)
                with dve.Fori(1, GROUPS - 1) as g:
                    group(g, g - 1, True)
                last = GROUPS - 1
                group(last, last - 1, False)
                normalise(last, 2)
                normalise(last, 3)
                add_residual(last)
                norm_ffn(last)
                router_top(last)
                router_weights(last)

            @block.gpsimd
            def _(pool):
                def rope_sum(g, j):
                    n = PAIRS * g + j
                    if not (zero(g) and j < 2):
                        pool.wait_ge(qk_lo_done, 3 * (n - 2) + 3)
                    for k, to in enumerate((q_sum, k_sum)):
                        pool.wait_ge(proj_left, ITEMS * g + FIRST[j] + 2 * k + 2)
                        nc.gpsimd.tensor_tensor(to[:, j % 2, :], term[:, 2 * k, :], term[:, 2 * k + 1, :], ALU.add).then_inc(rope_done, 1)

                def low(g, j):
                    n = PAIRS * g + j
                    pool.wait_ge(rope_done, 2 * n + 2)
                    pool.wait_ge(qk_hi_done, 3 * n + 1)
                    nc.gpsimd.tensor_tensor(q_lo[:, j, :], q_sum[:, j % 2, :], q_hi[:, j, :], ALU.subtract).then_inc(qk_lo_done, 1)
                    for h in range(2):
                        rows = slice(TAB * h, TAB * h + TAB)
                        pool.wait_ge(qk_hi_done, 3 * n + 2 + h)
                        if h:
                            pool.wait_ge(qk_lo_done, 3 * n + 2)
                        nc.gpsimd.tensor_tensor(k_lo[rows, j, :, TAB * h:TAB * h + N],
                                                k_sum[rows, j % 2, :].rearrange("p (b n) -> p b n", b=GI),
                                                k_hi[rows, j, :, TAB * h:TAB * h + N], ALU.subtract).then_inc(qk_lo_done, 1)
                    pool.wait_ge(qk_lo_done, 3 * n + 3)

                def negate(g, j):
                    n = PAIRS * g + j
                    pool.wait_ge(max_done, n + 1)
                    if not (zero(g) and j < 2):
                        pool.wait_ge(logits_done, n - 1)
                    nc.gpsimd.tensor_tensor(neg_max[:, j % 2, :].rearrange("p (b n) -> p b n", b=GI),
                                            row_max[:, j % 2, :].unsqueeze(2).broadcast_to([128, GI, N]), neg_id, ALU.mult).then_inc(neg_done, 1)

                def group(g):
                    rope_sum(g, 0)
                    low(g, 0)
                    rope_sum(g, 1)
                    low(g, 1)
                    rope_sum(g, 2)
                    negate(g, 0)
                    low(g, 2)
                    rope_sum(g, 3)
                    negate(g, 1)
                    low(g, 3)
                    negate(g, 2)
                    negate(g, 3)

                for t in (k_hi, k_lo, v_hi, v_lo):
                    nc.gpsimd.memset(t[:, :, :, :].bitcast(F32), 0.0).then_inc(s_fill, 1)
                pool.wait_ge(s_fill, 4)
                group(0)
                with pool.Fori(1, GROUPS) as g:
                    group(g)

        two.close()

        with ExitStack() as own:
            DEPTH = 4
            LEAD = 4
            f_hi = sb("f_hi", [128, TOKENS], F32R, own)
            f_lo = sb("f_lo", [128, TOKENS], F32R, own)
            w2_sb = sb("w2_sb", [128, FC, D], F32, own)
            scaled = sb("scaled", [128, DEPTH, 2 * T], F32, own)
            act_out = sb("act_out", [128, DEPTH, 2 * T], F32, own)
            hidden = sb("hidden", [128, DEPTH, T], F32, own)
            result = sb("result", [128, 2, T], F32, own)

            W2_PARTS = 8
            w2_in = [sem(f"w2_in{i}") for i in range(W2_PARTS)]
            f_hi_done = sem("f_hi_done")
            f_split = sem("f_split")
            up_done = sem("up_done")
            scaled_done = sem("scaled_done")
            gelu_done = sem("gelu_done")
            hidden_done = sem("hidden_done")
            down_done = sem("down_done")
            result_done = sem("result_done")
            stored = sem("stored")

            SUM = 7
            block = own.enter_context(nc.Block())

            @block.tensor
            def _(pe):
                def up(g, c):
                    n = FC * g + c
                    if c == 0:
                        pe.wait_ge(f_split, g + 1)
                    if not (isinstance(g, int) and n < DEPTH):
                        pe.wait_ge(scaled_done, n - DEPTH + 1)
                    xs = bass.ds(g * T, T)
                    to = psum[:, c % DEPTH, 0:T]
                    ws = slice(c * D, c * D + D)
                    pe.matmul(to, w1_hi[:, ws], f_hi[:, xs], start=True, stop=False)
                    pe.matmul(to, w1_hi[:, ws], f_lo[:, xs], start=False, stop=False)
                    pe.matmul(to, w1_lo[:, ws], f_hi[:, xs], start=False, stop=True).then_inc(up_done, 1)

                def down(g, c):
                    pe.wait_ge(hidden_done, FC * g + c + 1)
                    if isinstance(g, int) and g == 0 and c % (FC // W2_PARTS) == 0:
                        pe.wait_ge(w2_in[c // (FC // W2_PARTS)], 16)
                    if c == 0 and not (isinstance(g, int) and g == 0):
                        pe.wait_ge(result_done, g)
                    pe.matmul(psum[:, SUM, 0:T], w2_sb[:, c, :], hidden[:, c % DEPTH, :],
                              start=(c == 0), stop=(c == FC - 1)).then_inc(down_done, 1)

                for c in range(LEAD):
                    up(0, c)
                for c in range(LEAD, FC):
                    up(0, c)
                    down(0, c - LEAD)
                pe.wait_ge(w2_in[W2_PARTS - 1], 16)
                with pe.Fori(1, GROUPS) as g:
                    for c in range(FC):
                        up(g, c)
                        if c < LEAD:
                            down(g - 1, FC - LEAD + c)
                        else:
                            down(g, c - LEAD)
                for c in range(FC - LEAD, FC):
                    down(GROUPS - 1, c)

            @block.vector
            def _(dve):
                def split(g):
                    here = bass.ds(g * T, T)
                    nc.vector.tensor_copy(f_hi[:, here], normed[:, here]).then_inc(f_hi_done, 1)
                    dve.wait_ge(f_hi_done, g + 1)
                    nc.vector.tensor_tensor(f_lo[:, here], normed[:, here], f_hi[:, here].bitcast(F32), ALU.subtract).then_inc(f_split, 1)

                def scale(g, c):
                    n = FC * g + c
                    dve.wait_ge(up_done, n + 1)
                    if not (isinstance(g, int) and n < DEPTH):
                        dve.wait_ge(gelu_done, n - DEPTH + 1)
                    nc.vector.tensor_tensor(scaled[:, c % DEPTH, :].rearrange("p (i t) -> p i t", i=2),
                                            psum[:, c % DEPTH, 0:T].unsqueeze(1).broadcast_to([128, 2, T]),
                                            scales[:, bass.ds(g, 1), :].rearrange("p a (i t) -> p (a i) t", i=2),
                                            ALU.mult).then_inc(scaled_done, 1)

                def finish(g):
                    dve.wait_ge(down_done, FC * (g + 1))
                    if not (isinstance(g, int) and g == 0):
                        dve.wait_ge(stored, 16 * g)
                    nc.vector.scalar_tensor_tensor(out=result[:, 0, :], in0=psum[:, SUM, 0:T], scalar=b2_sum,
                                                   in1=residual[:, bass.ds(g * T, T)], op0=ALU.add, op1=ALU.add).then_inc(result_done, 1)

                split(0)
                for c in range(FC):
                    scale(0, c)
                    if c == FC // 2:
                        split(1)
                with dve.Fori(1, GROUPS - 1) as g:
                    for c in range(FC):
                        scale(g, c)
                        if c == LEAD:
                            finish(g - 1)
                        if c == FC // 2:
                            split(g + 1)
                last = GROUPS - 1
                for c in range(FC):
                    scale(last, c)
                    if c == LEAD:
                        finish(last - 1)
                finish(last)

            @block.scalar
            def _(act):
                def gelu(g, c):
                    n = FC * g + c
                    act.wait_ge(scaled_done, n + 1)
                    if not (isinstance(g, int) and n < DEPTH):
                        act.wait_ge(hidden_done, n - DEPTH + 1)
                    nc.scalar.activation(act_out[:, c % DEPTH, :], scaled[:, c % DEPTH, :], ACT.Gelu,
                                         bias=vec[:, V_B1 + c:V_B1 + c + 1]).then_inc(gelu_done, 1)

                act.preload_act_table(ACT.Gelu)
                for c in range(FC):
                    gelu(0, c)
                with act.Fori(1, GROUPS) as g:
                    for c in range(FC):
                        gelu(g, c)

            @block.gpsimd
            def _(pool):
                def add(g, c):
                    n = FC * g + c
                    pool.wait_ge(gelu_done, n + 1)
                    if not (isinstance(g, int) and n < DEPTH):
                        pool.wait_ge(down_done, n - DEPTH + 1)
                    nc.gpsimd.tensor_tensor(hidden[:, c % DEPTH, :], act_out[:, c % DEPTH, 0:T], act_out[:, c % DEPTH, T:2 * T],
                                            ALU.add).then_inc(hidden_done, 1)

                for c in range(FC):
                    add(0, c)
                with pool.Fori(1, GROUPS) as g:
                    for c in range(FC):
                        add(g, c)

            @block.sync
            def _(sp):
                for i in range(W2_PARTS):
                    part = slice(i * FC // W2_PARTS, (i + 1) * FC // W2_PARTS)
                    sp.dma_start(w2_sb[:, part, :], w2[:, part, :]).then_inc(w2_in[i], 16)
                with sp.Fori(0, GROUPS) as g:
                    sp.wait_ge(result_done, g + 1)
                    sp.dma_start(out[:, bass.ds(g * T, T)], result[:, 0, :]).then_inc(stored, 16)
                sp.wait_ge(stored, 16 * GROUPS)


def _constants():
    c = np.zeros((128, C_WIDTH), np.float32)
    c[:, C_IDENT:C_IDENT + 128] = np.eye(128)
    c[:, C_CENTRE:C_CENTRE + 128] = np.eye(128) - 1.0 / D
    p = np.arange(128)
    same = (p[:, None] // TAB) == (p[None, :] // TAB)
    real = (p % TAB) < N
    c[:, C_HEADS:C_HEADS + 128] = same & real[None, :] & real[:, None]
    c[:, C_HEADROWS:C_HEADROWS + 128] = same & real[:, None]
    c[:, C_NEGID:C_NEGID + N] = -1.0 * ((p[:, None] % TAB) == np.arange(N)[None, :])
    inv_freq = (1.0 / np.float32(10000.0) ** (np.arange(0, HD, 2, dtype=np.float32) / np.float32(HD))).astype(np.float32)
    angle = (inv_freq[(p % HD) // 2][:, None] * np.arange(N, dtype=np.float32)[None, :]).astype(np.float32)
    sign = np.where(p % 2 == 0, -1.0, 1.0)[:, None]
    c[:, C_COS:C_COS + T] = np.tile(np.cos(angle), (1, GI))
    c[:, C_SIN:C_SIN + T] = np.tile(sign * np.sin(angle), (1, GI))
    return c


def _patch_order():
    return [(a, b) for a in range(-1, PATCH + 1) for b in range(-1, PATCH + 1)
            if not (a in (-1, PATCH) and b in (-1, PATCH))]


def _layout_patches(x):
    side = SIDE * PATCH
    padded = np.zeros((IMAGES, side + 2, side + 2, CH), x.dtype)
    padded[:, 1:-1, 1:-1] = x
    order = np.array(_patch_order()) + 1
    starts = PATCH * np.arange(SIDE)[:, None]
    rows, columns = starts + order[:, 0], starts + order[:, 1]
    taken = padded[:, rows[:, None, :], columns[None, :, :], :]
    taken = taken.reshape(GROUPS, T, KC, KP)
    return np.ascontiguousarray(taken.transpose(0, 3, 2, 1))


def _layout_conv(w):
    out = np.zeros((5, PATCH + 2, PATCH + 2, CH, D), w.dtype)
    w = w.reshape(PATCH, PATCH, 5, CH, D)
    for s, (dy, dx) in enumerate(((0, 0), (0, -1), (0, 1), (-1, 0), (1, 0))):
        out[s, 1 + dy:1 + dy + PATCH, 1 + dx:1 + dx + PATCH] = w[:, :, s]
    order = np.array(_patch_order()) + 1
    out = out[:, order[:, 0], order[:, 1]].reshape(5, KC, KP, D)
    return np.ascontiguousarray(out.transpose(0, 2, 1, 3).reshape(5, KP, KC * D))


def kernel(x, L0_tok_conv_w, L0_tok_conv_b, L0_tok_gamma, L0_tok_beta, L0_tok_dense_w, L0_tok_dense_b,
           L0_attn_gamma, L0_attn_w_qkv, L0_attn_w_out, L0_ffn_Wg, L0_ffn_W1, L0_ffn_b1, L0_ffn_W2, L0_ffn_b2):
    import concourse.bacc as bacc
    from concourse.bass_utils import run_bass_kernel_spmd

    def arr(a):
        return np.asarray(a)

    vectors = np.zeros((128, V_WIDTH), np.float32)
    for col, v in ((V_CONVB, L0_tok_conv_b), (V_GAMMA, L0_tok_gamma), (V_BETA, L0_tok_beta),
                   (V_DENSEB, L0_tok_dense_b), (V_ATTNG, L0_attn_gamma)):
        vectors[:, col] = arr(v)
    vectors[:, V_B1:V_B1 + FC] = arr(L0_ffn_b1).reshape(FC, D).T
    vectors[:, V_B2:V_B2 + EXPERTS] = arr(L0_ffn_b2).T
    arrays = {
        "patches": _layout_patches(arr(x)),
        "shifted_w": _layout_conv(arr(L0_tok_conv_w)),
        "vectors": vectors,
        "dense_w": arr(L0_tok_dense_w),
        "w_qkv": arr(L0_attn_w_qkv),
        "w_out": arr(L0_attn_w_out).reshape(PAIRS, D, D).transpose(1, 0, 2),
        "w_gate": arr(L0_ffn_Wg),
        "w1": arr(L0_ffn_W1).transpose(1, 0, 2).reshape(D, EXPERTS * DFF),
        "w2": arr(L0_ffn_W2).reshape(FC, D, D).transpose(1, 0, 2),
        "consts": _constants(),
    }
    arrays = {k: np.ascontiguousarray(v) for k, v in arrays.items()}
    nc = bacc.Bacc("TRN2", target_bir_lowering=False, num_devices=1)
    ins = [nc.dram_tensor(f"in_{k}", v.shape, mybir.dt.from_np(v.dtype), kind="ExternalInput").ap() for k, v in arrays.items()]
    out = nc.dram_tensor("out_0", (D, TOKENS), F32, kind="ExternalOutput").ap()
    vit_tower(nc, *ins, out)
    r = run_bass_kernel_spmd(nc, [{f"in_{k}": v for k, v in arrays.items()}], core_ids=[0])
    got = r.results[0]["out_0"]
    return np.ascontiguousarray(got.T).reshape(IMAGES, N, D)
```

```python
from contextlib import ExitStack

import numpy as np

import concourse.bass as bass
from concourse import mybir

F32 = mybir.dt.float32
F32R = mybir.dt.float32r
F16 = mybir.dt.float16
ALU = mybir.AluOpType
ACT = mybir.ActivationFunctionType
AX_X = mybir.AxisListType.X

D = 128
N = 49
IMAGES = 64
GROUPS = 8
GI = IMAGES // GROUPS
T = GI * N
TOKENS = IMAGES * N
PATCH, SIDE, CH = 16, 7, 3
K_CONV = 960
KC = 8
KP = K_CONV // KC
PARTS = 4
PC = KC // PARTS
PAIRS = 4
HD = 64
QT = T // 4
EXPERTS, DFF = 8, 512
FC = EXPERTS * DFF // D
W1_PART = EXPERTS * DFF // GROUPS
TAB = 64
LOG_SCALE = 2.0 ** 20
RMS_FLOOR = (1e-8 ** 2 / D) * 1e-5

C_IDENT, C_CENTRE, C_HEADS, C_HEADROWS, C_NEGID, C_COS, C_SIN = 0, 128, 256, 384, 512, 561, 953
C_WIDTH = 953 + 392
V_CONVB, V_GAMMA, V_BETA, V_DENSEB, V_ATTNG, V_B1, V_B2 = 0, 1, 2, 3, 4, 5, 37
V_WIDTH = 45


def vit_tower(nc, patches, shifted_w, vectors, dense_w, w_qkv, w_out, w_gate, w1, w2, consts, out):
    with ExitStack() as ctx:
        def sem(name):
            return ctx.enter_context(nc.semaphore(name))

        def sb(name, shape, dt=F32, scope=ctx):
            return scope.enter_context(nc.sbuf_tensor(name, shape, dt))

        psum = ctx.enter_context(nc.psum_tensor("psum", [128, 8, 512], F32))
        const = sb("const", [128, C_WIDTH])
        vec = sb("vec", [128, V_WIDTH])
        ident = const[:, C_IDENT:C_IDENT + 128]
        centre = const[:, C_CENTRE:C_CENTRE + 128]
        ones = sb("ones", [128, 128])
        ones_mean = sb("ones_mean", [128, 128])
        cols = sb("cols", [128, 4])
        eps_conv, eps_ln, ln_shift, b2_sum = (cols[:, i:i + 1] for i in range(4))
        residual = sb("residual", [128, TOKENS])
        normed = sb("normed", [128, TOKENS])
        scales = sb("scales", [128, GROUPS, 2 * T])
        w1_hi = sb("w1_hi", [128, FC * D], F32R)
        w1_lo = sb("w1_lo", [128, FC * D], F32R)

        two = ctx.enter_context(ExitStack())
        wqk_hi = sb("wqk_hi", [128, 2, 8 * D], F32R, two)
        wqk_lo = sb("wqk_lo", [128, 2, 8 * D], F32R, two)
        wv_hi = sb("wv_hi", [128, 4 * D], F32R, two)
        wv_lo = sb("wv_lo", [128, 4 * D], F32R, two)
        wo_sb = sb("wo_sb", [128, PAIRS, D], F32, two)
        wg_sb = sb("wg_sb", [128, EXPERTS], F32, two)
        heads_r = sb("heads_r", [128, 128], F32R, two)
        headrows = sb("headrows", [128, 128], F16, two)

        with ExitStack() as own:
            shifts = sb("shifts", [KP, PARTS, 5, KC * D // PARTS], F32, own)
            conv_w = sb("conv_w", [KP, KC, D], F32, own)
            conv_mean = sb("conv_mean", [KP, KC], F32, own)
            patch = sb("patch", [KP, KC, T], F32, own)
            dense_raw = sb("dense_raw", [128, D], F32, own)
            dense_g = sb("dense_g", [128, D], F32, own)
            dense_c = sb("dense_c", [128, D], F32, own)
            dense_mean = sb("dense_mean", [128, 1], F32, own)
            conv_bc = sb("conv_bc", [128, 1], F32, own)
            dense_b = sb("dense_b", [128, 1], F32, own)
            dense_bc = sb("dense_bc", [128, 1], F32, own)
            raw = scales[:, :, :].rearrange("p g t -> p (g t)")
            w1_raw = raw[:, 0:FC * D]
            qkv_raw = raw[:, FC * D:FC * D + 12 * D]
            y = sb("y", [128, T], F32, own)
            square = sb("square", [128, T], F32, own)
            log1 = sb("log1", [128, T], F32, own)
            rstd1 = sb("rstd1", [128, T], F32, own)
            y_normed = sb("y_normed", [128, T], F32, own)
            square2 = sb("square2", [128, T], F32, own)
            floored = sb("floored", [128, T], F32, own)
            log2 = sb("log2", [128, T], F32, own)
            rstd2 = sb("rstd2", [128, T], F32, own)

            small_in = sem("small_in")
            shifts_in = [sem(f"shifts_in{c}") for c in range(PARTS)]
            qkv_in = sem("qkv_in")
            attn_in = sem("attn_in")
            ffn_in = sem("ffn_in")
            patch_in = [sem(f"patch_in{c}") for c in range(PARTS)]
            fills = sem("fills")
            fold = sem("fold")
            wprep = sem("wprep")
            conv_ready = sem("conv_ready")
            dense_ready = sem("dense_ready")
            bias_mm = sem("bias_mm")
            bias_ready = sem("bias_ready")
            qkv_steps = sem("qkv_steps")
            w1_hi_done = sem("w1_hi_done")
            qkv_hi_done = sem("qkv_hi_done")
            swap_done = sem("swap_done")
            conv_done = sem("conv_done")
            y_out = sem("y_out")
            var1_done = sem("var1_done")
            log1_done = sem("log1_done")
            rstd1_done = sem("rstd1_done")
            y_normed_done = sem("y_normed_done")
            dense_done = sem("dense_done")
            square2_done = sem("square2_done")
            residual_done = sem("residual_done")
            var2_done = sem("var2_done")
            floored_done = sem("floored_done")
            log2_done = sem("log2_done")
            rstd2_done = sem("rstd2_done")
            normed_done = sem("normed_done")

            Y, VAR1, PLAIN, CENTRED, VAR2, BIAS = (psum[:, i, 0:T] for i in range(6))

            block = own.enter_context(nc.Block())

            @block.sync
            def _(sp):
                for c in range(PARTS):
                    sp.dma_start(shifts[:, c, :, :], shifted_w[:, c, :, :]).then_inc(shifts_in[c], 16)
                    sp.dma_start(patch[:, PC * c:PC * c + PC, :], patches[0, :, PC * c:PC * c + PC, :]).then_inc(patch_in[c], 16)
                sp.dma_start(qkv_raw, w_qkv).then_inc(qkv_in, 16)
                sp.dma_start(w1_raw, w1).then_inc(ffn_in, 16)
                with sp.Fori(1, GROUPS) as g:
                    for c in range(PARTS):
                        sp.wait_ge(conv_done, (g - 1) * (PARTS) + c + 1)
                        sp.dma_start(patch[:, PC * c:PC * c + PC, :],
                                     patches[bass.ds(g, 1), :, PC * c:PC * c + PC, :].rearrange("a p c t -> p (a c) t")).then_inc(patch_in[c], 16)

            @block.scalar
            def _(act):
                act.preload_act_table_set("natural_log_exp_and_others")
                act.dma_start(vec[:, :], vectors).then_inc(small_in, 16)
                act.dma_start(const[:, :], consts).then_inc(small_in, 16)
                act.dma_start(dense_raw[:, :], dense_w).then_inc(small_in, 16)
                act.dma_start(wo_sb[:, :, :], w_out).then_inc(attn_in, 16)
                act.dma_start(wg_sb[:, :], w_gate).then_inc(attn_in, 16)

                def leave_conv(g):
                    act.wait_ge(conv_done, (g + 1) * (PARTS))
                    if not (isinstance(g, int) and g == 0):
                        act.wait_ge(var1_done, g)
                    nc.scalar.activation(square[:, :], Y, ACT.Square, bias=conv_bc[:, 0:1]).then_inc(y_out, 1)
                    if not (isinstance(g, int) and g == 0):
                        act.wait_ge(y_normed_done, g)
                    nc.scalar.activation(y[:, :], Y, ACT.Identity, bias=conv_bc[:, 0:1]).then_inc(y_out, 1)

                def norm1(g):
                    act.wait_ge(var1_done, g + 1)
                    nc.scalar.activation(log1[:, :], VAR1, ACT.Ln, bias=eps_conv).then_inc(log1_done, 1)
                    act.wait_ge(log1_done, g + 1)
                    nc.scalar.activation(rstd1[:, :], log1[:, :], ACT.Exp, scale=-0.5).then_inc(rstd1_done, 1)

                def leave_dense(g):
                    act.wait_ge(dense_done, 2 * g + 1)
                    nc.scalar.activation(square2[:, :], CENTRED, ACT.Square, bias=dense_bc[:, 0:1]).then_inc(square2_done, 1)
                    act.wait_ge(dense_done, 2 * g + 2)
                    nc.scalar.activation(residual[:, bass.ds(g * T, T)], PLAIN, ACT.Identity, bias=dense_b[:, 0:1]).then_inc(residual_done, 1)

                def norm2(g):
                    act.wait_ge(floored_done, g + 1)
                    nc.scalar.activation(log2[:, :], floored[:, :], ACT.Ln, scale=LOG_SCALE).then_inc(log2_done, 1)
                    act.wait_ge(log2_done, g + 1)
                    if not (isinstance(g, int) and g == 0):
                        act.wait_ge(normed_done, g)
                    nc.scalar.activation(rstd2[:, :], log2[:, :], ACT.Exp, scale=-0.5, bias=ln_shift).then_inc(rstd2_done, 1)

                act.wait_ge(bias_ready, 3)
                leave_conv(0)
                norm1(0)
                act.wait_ge(qkv_steps, 1)
                nc.scalar.activation(wqk_hi[:, 0, :], qkv_raw[:, 0:8 * D], ACT.Copy).then_inc(qkv_hi_done, 1)
                nc.scalar.activation(wv_hi[:, :], qkv_raw[:, 8 * D:12 * D], ACT.Copy).then_inc(qkv_hi_done, 1)
                act.wait_ge(ffn_in, 16)
                with act.Fori(1, GROUPS) as g:
                    leave_dense(g - 1)
                    leave_conv(g)
                    norm2(g - 1)
                    norm1(g)
                    here = bass.ds((g - 1) * W1_PART, W1_PART)
                    nc.scalar.activation(w1_hi[:, here], w1_raw[:, here], ACT.Copy).then_inc(w1_hi_done, 1)
                here = bass.ds((GROUPS - 1) * W1_PART, W1_PART)
                nc.scalar.activation(w1_hi[:, here], w1_raw[:, here], ACT.Copy).then_inc(w1_hi_done, 1)
                leave_dense(GROUPS - 1)
                norm2(GROUPS - 1)

            @block.vector
            def _(dve):
                nc.vector.memset(ones[:, :], 1.0).then_inc(fills, 1)
                nc.vector.memset(ones_mean[:, :], 1.0 / D).then_inc(fills, 1)
                nc.vector.memset(eps_conv, 1e-3).then_inc(fills, 1)
                nc.vector.memset(eps_ln, 1e-5).then_inc(fills, 1)
                nc.vector.memset(ln_shift, 0.5 * float(np.log(LOG_SCALE))).then_inc(fills, 1)
                for c in range(PARTS):
                    here = conv_w[:, PC * c:PC * c + PC, :]
                    mean = conv_mean[:, PC * c:PC * c + PC]
                    shift = [shifts[:, c, k, :].rearrange("p (c d) -> p c d", c=PC) for k in range(5)]
                    at = 6 * c
                    dve.wait_ge(shifts_in[c], 16)
                    nc.vector.tensor_tensor(here, shift[0], shift[1], ALU.add).then_inc(fold, 1)
                    for k in range(2, 5):
                        dve.wait_ge(fold, at + k - 1)
                        nc.vector.tensor_tensor(here, here, shift[k], ALU.add).then_inc(fold, 1)
                    dve.wait_ge(fold, at + 4)
                    nc.vector.tensor_reduce(mean, here, AX_X, ALU.add).then_inc(fold, 1)
                    dve.wait_ge(fold, at + 5)
                    nc.vector.tensor_scalar(mean, mean, 1.0 / D, None, ALU.mult).then_inc(fold, 1)
                    dve.wait_ge(fold, at + 6)
                    nc.vector.tensor_tensor(here, here, mean.unsqueeze(2).broadcast_to([KP, PC, D]), ALU.subtract).then_inc(conv_ready, 1)
                dve.wait_ge(small_in, 48)
                nc.vector.tensor_scalar(dense_g[:, :], dense_raw[:, :], vec[:, V_GAMMA:V_GAMMA + 1], None, ALU.mult).then_inc(wprep, 1)
                dve.wait_ge(wprep, 1)
                nc.vector.tensor_reduce(dense_mean[:, :], dense_g[:, :], AX_X, ALU.add).then_inc(wprep, 1)
                dve.wait_ge(wprep, 2)
                nc.vector.tensor_scalar(dense_mean[:, :], dense_mean[:, :], 1.0 / D, None, ALU.mult).then_inc(wprep, 1)
                dve.wait_ge(wprep, 3)
                nc.vector.tensor_scalar(dense_c[:, :], dense_g[:, :], dense_mean[:, 0:1], None, ALU.subtract).then_inc(dense_ready, 1)
                dve.wait_ge(bias_mm, 1)
                nc.vector.tensor_copy(conv_bc[:, :], BIAS[:, 0:1]).then_inc(bias_ready, 1)
                nc.vector.tensor_tensor(dense_b[:, :], BIAS[:, 1:2], vec[:, V_DENSEB:V_DENSEB + 1], ALU.add).then_inc(bias_ready, 1)
                dve.wait_ge(bias_mm, 2)
                nc.vector.tensor_copy(dense_bc[:, :], BIAS[:, 2:3]).then_inc(bias_ready, 1)
                nc.vector.tensor_copy(headrows[:, :], const[:, C_HEADROWS:C_HEADROWS + 128]).then_inc(wprep, 1)
                nc.vector.tensor_copy(heads_r[:, :], const[:, C_HEADS:C_HEADS + 128]).then_inc(wprep, 1)
                nc.vector.tensor_reduce(b2_sum, vec[:, V_B2:V_B2 + EXPERTS], AX_X, ALU.add).then_inc(wprep, 1)
                dve.wait_ge(wprep, 6)
                nc.vector.tensor_scalar(b2_sum, b2_sum, 2.0, None, ALU.mult).then_inc(wprep, 1)

                def scale1(g):
                    dve.wait_ge(rstd1_done, g + 1)
                    dve.wait_ge(y_out, 2 * g + 2)
                    if not (isinstance(g, int) and g == 0):
                        dve.wait_ge(dense_done, 2 * g)
                    nc.vector.tensor_tensor(y_normed[:, :], y[:, :], rstd1[:, :], ALU.mult).then_inc(y_normed_done, 1)

                def scale2(g):
                    dve.wait_ge(var2_done, g + 1)
                    if not (isinstance(g, int) and g == 0):
                        dve.wait_ge(log2_done, g)
                    nc.vector.tensor_scalar(floored[:, :], VAR2, RMS_FLOOR, None, ALU.max).then_inc(floored_done, 1)
                    dve.wait_ge(rstd2_done, g + 1)
                    nc.vector.scalar_tensor_tensor(out=normed[:, bass.ds(g * T, T)], in0=CENTRED, scalar=dense_bc[:, 0:1],
                                                   in1=rstd2[:, :], op0=ALU.add, op1=ALU.mult).then_inc(normed_done, 1)

                scale1(0)
                for part, src in enumerate((wqk_hi, wqk_lo)):
                    if part == 0:
                        dve.wait_ge(qkv_hi_done, 2)
                    else:
                        dve.wait_ge(qkv_steps, 3)
                    pairs = src[:, :, :].bitcast(F32).rearrange("p s (c e) -> p s c e", e=2)
                    outs = src[:, :, :].rearrange("p s (c e) -> p s c e", e=2)
                    nc.vector.tensor_copy(outs[:, 1, :, 0], pairs[:, 0, :, 1]).then_inc(swap_done, 1)
                    nc.vector.tensor_copy(outs[:, 1, :, 1], pairs[:, 0, :, 0]).then_inc(swap_done, 1)
                with dve.Fori(1, GROUPS) as g:
                    scale2(g - 1)
                    scale1(g)
                scale2(GROUPS - 1)

            @block.gpsimd
            def _(pool):
                pool.wait_ge(qkv_in, 16)
                pool.wait_ge(small_in, 48)
                nc.gpsimd.tensor_scalar(qkv_raw, qkv_raw, vec[:, V_ATTNG:V_ATTNG + 1], None, ALU.mult).then_inc(qkv_steps, 1)
                pool.wait_ge(qkv_hi_done, 2)
                nc.gpsimd.tensor_tensor(wv_lo[:, :], qkv_raw[:, 8 * D:12 * D], wv_hi[:, :].bitcast(F32), ALU.subtract).then_inc(qkv_steps, 1)
                nc.gpsimd.tensor_tensor(wqk_lo[:, 0, :], qkv_raw[:, 0:8 * D], wqk_hi[:, 0, :].bitcast(F32), ALU.subtract).then_inc(qkv_steps, 1)
                with pool.Fori(0, GROUPS) as i:
                    pool.wait_ge(w1_hi_done, i + 1)
                    here = bass.ds(i * W1_PART, W1_PART)
                    nc.gpsimd.tensor_tensor(w1_lo[:, here], w1_raw[:, here], w1_hi[:, here].bitcast(F32), ALU.subtract).then_inc(qkv_steps, 1)

            @block.tensor
            def _(pe):
                def conv(g, first, last):
                    if first == 0 and not (isinstance(g, int) and g == 0):
                        pe.wait_ge(y_out, 2 * g)
                    for c in range(first, last):
                        if c % PC == 0:
                            pe.wait_ge(patch_in[c // PC], 16 * g + 16)
                            if isinstance(g, int) and g == 0:
                                pe.wait_ge(conv_ready, c // PC + 1)
                        mm = pe.matmul(Y, conv_w[:, c, :], patch[:, c, :], start=(c == 0), stop=(c == KC - 1))
                        if c % PC == PC - 1:
                            mm.then_inc(conv_done, 1)

                def variance1(g):
                    pe.wait_ge(y_out, 2 * g + 1)
                    if not (isinstance(g, int) and g == 0):
                        pe.wait_ge(log1_done, g)
                    pe.matmul(VAR1, ones_mean[:, :], square[:, :], start=True, stop=True).then_inc(var1_done, 1)

                def dense(g):
                    pe.wait_ge(y_normed_done, g + 1)
                    if not (isinstance(g, int) and g == 0):
                        pe.wait_ge(normed_done, g)
                    pe.matmul(CENTRED, dense_c[:, :], y_normed[:, :], start=True, stop=True).then_inc(dense_done, 1)
                    if not (isinstance(g, int) and g == 0):
                        pe.wait_ge(residual_done, g)
                    pe.matmul(PLAIN, dense_g[:, :], y_normed[:, :], start=True, stop=True).then_inc(dense_done, 1)

                def variance2(g):
                    pe.wait_ge(square2_done, g + 1)
                    if not (isinstance(g, int) and g == 0):
                        pe.wait_ge(floored_done, g)
                    pe.matmul(VAR2, ones_mean[:, :], square2[:, :], start=True, stop=True).then_inc(var2_done, 1)

                conv(0, 0, KC)
                pe.wait_ge(dense_ready, 1)
                pe.matmul(BIAS[:, 0:1], centre, vec[:, V_CONVB:V_CONVB + 1], start=True, stop=True)
                pe.matmul(BIAS[:, 1:2], dense_raw[:, :], vec[:, V_BETA:V_BETA + 1], start=True, stop=True).then_inc(bias_mm, 1)
                pe.wait_ge(bias_ready, 2)
                pe.matmul(BIAS[:, 2:3], centre, dense_b[:, :], start=True, stop=True).then_inc(bias_mm, 1)
                pe.wait_ge(fills, 5)
                with pe.Fori(1, GROUPS) as g:
                    conv(g, 0, 3)
                    variance1(g - 1)
                    conv(g, 3, 6)
                    dense(g - 1)
                    conv(g, 6, KC)
                    variance2(g - 1)
                variance1(GROUPS - 1)
                dense(GROUPS - 1)
                variance2(GROUPS - 1)

        with ExitStack() as own:
            x_hi = sb("x_hi", [128, T], F32R, own)
            x_lo = sb("x_lo", [128, T], F32R, own)
            xv_hi = sb("xv_hi", [128, GI, TAB], F32R, own)
            xv_lo = sb("xv_lo", [128, GI, TAB], F32R, own)
            term = sb("term", [128, 4, T], F32, own)
            q_sum = sb("q_sum", [128, 2, T], F32, own)
            k_sum = sb("k_sum", [128, 2, T], F32, own)
            q_hi = sb("q_hi", [128, PAIRS, T], F16, own)
            q_lo = sb("q_lo", [128, PAIRS, T], F16, own)
            k_hi = sb("k_hi", [128, PAIRS, GI, 2 * TAB], F16, own)
            k_lo = sb("k_lo", [128, PAIRS, GI, 2 * TAB], F16, own)
            v_hi = [sb(f"v_hi{i}", [128, GI, PAIRS, D], F16, own) for i in range(2)]
            v_lo = [sb(f"v_lo{i}", [128, GI, PAIRS, D], F16, own) for i in range(2)]
            row_max = sb("row_max", [128, 2, GI], F32, own)
            neg_max = sb("neg_max", [128, 2, T], F32R, own)
            prob = sb("prob", [128, 2, T], F32, own)
            prob_hi = sb("prob_hi", [128, 2, T], F16, own)
            prob_lo = sb("prob_lo", [128, 2, T], F16, own)
            inv_den = sb("inv_den", [128, T], F32, own)
            heads_out = sb("heads_out", [128, PAIRS, T], F32, own)
            square3 = sb("square3", [128, T], F32, own)
            rstd3 = square3
            ffn_x = sb("ffn_x", [128, T], F32, own)
            top = sb("top", [QT, 4, 8], F32, own)
            gap = sb("gap", [QT, 4], F32, own)
            ratio = sb("ratio", [QT, 4], F32, own)
            den2 = sb("den2", [QT, 4], F32, own)
            weight = sb("weight", [QT, 2, 4], F32, own)
            weight_diag = sb("weight_diag", [QT, 8, QT], F32, own)

            k_fill = sem("k_fill")
            v_fill = sem("v_fill")
            dve_fill = sem("dve_fill")
            x_hi_done = sem("x_hi_done")
            x_lo_done = sem("x_lo_done")
            xv_done = sem("xv_done")
            proj_done = sem("proj_done")
            bank_left = [sem(f"bank_left{i}") for i in range(3)]
            rope_done = sem("rope_done")
            qk_hi_done = sem("qk_hi_done")
            qk_lo_done = sem("qk_lo_done")
            v_hi_done = sem("v_hi_done")
            scores_done = sem("scores_done")
            neg_done = sem("neg_done")
            logits_done = sem("logits_done")
            prob_done = sem("prob_done")
            prob_lo_done = sem("prob_lo_done")
            den_done = sem("den_done")
            pv_done = sem("pv_done")
            log_den_done = sem("log_den_done")
            inv_done = sem("inv_done")
            heads_done = sem("heads_done")
            attn_done = sem("attn_done")
            h1_done = sem("h1_done")
            centre_done = sem("centre_done")
            square3_done = sem("square3_done")
            var3_done = sem("var3_done")
            log3_done = sem("log3_done")
            rstd3_done = sem("rstd3_done")
            ffn_x_done = sem("ffn_x_done")
            router_done = sem("router_done")
            ffn_in_done = sem("ffn_in_done")
            top_done = sem("top_done")
            small_done = sem("small_done")
            ratio_done = sem("ratio_done")
            diag_done = sem("diag_done")
            spread_done = sem("spread_done")
            scales_done = sem("scales_done")

            RING, LG, OUT, DEN, X0, X1 = 0, 3, 4, 5, 6, 7
            cos = const[:, C_COS:C_COS + T]
            sin = const[:, C_SIN:C_SIN + T]
            neg_id = const[:, C_NEGID:C_NEGID + N].unsqueeze(1).broadcast_to([128, GI, N])

            RING_ORDER = []
            for j in range(PAIRS):
                RING_ORDER += [("scores", (j - 1) % PAIRS)] + [("qk", 4 * j + n) for n in range(4)]
                if j < 2:
                    RING_ORDER += [("v", 2 * j), ("v", 2 * j + 1)]
            USES = len(RING_ORDER) // 3
            PROJ = [x for x in RING_ORDER if x[0] != "scores"]

            def ring(kind, n):
                return RING_ORDER.index((kind, n)) % 3

            def bank(kind, n):
                return psum[:, RING + ring(kind, n), :]

            def bank_turn(g, kind, n):
                return USES * g + RING_ORDER.index((kind, n)) // 3

            def score_turn(g, j):
                return bank_turn(g + 1 if j == PAIRS - 1 else g, "scores", j)

            def proj_count(g, kind, n):
                return len(PROJ) * g + PROJ.index((kind, n)) + 1

            def before(g, j, back):
                return (g, j - back) if j >= back else (g - 1, j - back + PAIRS)

            def known(g):
                return isinstance(g, int)

            block = own.enter_context(nc.Block())

            @block.tensor
            def _(pe):
                def claim(g, kind, n):
                    if not (known(g) and bank_turn(g, kind, n) <= 0):
                        pe.wait_ge(bank_left[ring(kind, n)], bank_turn(g, kind, n))

                def project(g, j):
                    if j == 0:
                        pe.wait_ge(x_lo_done, g + 1)
                    for n, (side, swapped) in enumerate(((0, 0), (0, 1), (1, 0), (1, 1))):
                        claim(g, "qk", 4 * j + n)
                        at = (side * PAIRS + j) * D
                        hi, lo = wqk_hi[:, swapped, at:at + D], wqk_lo[:, swapped, at:at + D]
                        to = bank("qk", 4 * j + n)[:, 0:T]
                        pe.matmul(to, hi, x_hi[:, 0:T], start=True, stop=False)
                        pe.matmul(to, hi, x_lo[:, 0:T], start=False, stop=False)
                        pe.matmul(to, lo, x_hi[:, 0:T], start=False, stop=True).then_inc(proj_done, 1)

                def values(g, p):
                    pe.wait_ge(xv_done, 2 * g + 2)
                    claim(g, "v", p)
                    hi = xv_hi[:, 2 * p:2 * p + 2, :].rearrange("p b n -> p (b n)")
                    lo = xv_lo[:, 2 * p:2 * p + 2, :].rearrange("p b n -> p (b n)")
                    to = bank("v", p)
                    pe.matmul(to, hi, wv_hi[:, :], start=True, stop=False)
                    pe.matmul(to, lo, wv_hi[:, :], start=False, stop=False)
                    pe.matmul(to, hi, wv_lo[:, :], start=False, stop=True).then_inc(proj_done, 1)

                def scores(g, j):
                    pe.wait_ge(qk_hi_done, 3 * (PAIRS * g + j) + 3)
                    claim(g + 1 if j == PAIRS - 1 else g, "scores", j)
                    pe.ldweights(headrows[:, :], tile_position=(0, 0))
                    to = bank("scores", j)
                    for b in range(GI):
                        for h in range(2):
                            rows = slice(TAB * h, TAB * h + TAB)
                            mm = pe.matmul(to[TAB * h:TAB * h + N, b * N:b * N + N],
                                           q_hi[rows, j, b * N:b * N + N],
                                           k_hi[rows, j, b, TAB * h:TAB * h + N], start=True, stop=True)
                    mm.then_inc(scores_done, 1)

                def logits(g, j):
                    n = PAIRS * g + j
                    pe.wait_ge(neg_done, n + 1)
                    pe.wait_ge(qk_lo_done, 3 * n + 3)
                    if not (known(g) and n == 0):
                        pe.wait_ge(prob_done, 2 * n)
                    pe.matmul(psum[:, LG, 0:T], heads_r[:, :], neg_max[:, j % 2, :], start=True, stop=False)
                    for b in range(GI):
                        to = psum[:, LG, b * N:b * N + N]
                        qs = slice(b * N, b * N + N)
                        pe.matmul(to, k_hi[:, j, b, :], q_hi[:, j, qs], start=False, stop=False)
                        pe.matmul(to, k_hi[:, j, b, :], q_lo[:, j, qs], start=False, stop=False)
                        mm = pe.matmul(to, k_lo[:, j, b, :], q_hi[:, j, qs], start=False, stop=(b == GI - 1))
                    mm.then_inc(logits_done, 1)

                def weigh(g, j, odd):
                    n = PAIRS * g + j
                    pe.wait_ge(prob_lo_done, n + 1)
                    if not (known(g) and n == 0):
                        pe.wait_ge(log_den_done, n)
                    pe.matmul(psum[:, DEN, 0:T], headrows[:, :], prob_hi[:, j % 2, :], start=True, stop=False)
                    pe.matmul(psum[:, DEN, 0:T], headrows[:, :], prob_lo[:, j % 2, :], start=False, stop=True).then_inc(den_done, 1)
                    if j == 0:
                        for p in range(GI // 2):
                            pe.wait_ge(bank_left[ring("v", p)], bank_turn(g, "v", p) + 1)
                    if not (known(g) and n == 0):
                        pe.wait_ge(heads_done, n)
                    for b in range(GI):
                        to = psum[:, OUT, b * N:b * N + N]
                        ps = slice(b * N, b * N + N)
                        pe.matmul(to, v_hi[odd][:, b, j, :], prob_hi[:, j % 2, ps], start=True, stop=False)
                        pe.matmul(to, v_hi[odd][:, b, j, :], prob_lo[:, j % 2, ps], start=False, stop=False)
                        mm = pe.matmul(to, v_lo[odd][:, b, j, :], prob_hi[:, j % 2, ps], start=False, stop=True)
                    mm.then_inc(pv_done, 1)

                def project_out(g):
                    pe.wait_ge(heads_done, PAIRS * (g + 1))
                    if not (known(g) and g == 0):
                        pe.wait_ge(scales_done, 2 * g)
                    for j in range(PAIRS):
                        mm = pe.matmul(psum[:, X0, 0:T], wo_sb[:, j, :], heads_out[:, j, :], start=(j == 0), stop=(j == PAIRS - 1))
                    mm.then_inc(attn_done, 1)

                def centre_h(g):
                    pe.wait_ge(h1_done, g + 1)
                    pe.matmul(psum[:, X1, 0:T], centre, residual[:, bass.ds(g * T, T)], start=True, stop=True).then_inc(centre_done, 1)

                def variance3(g):
                    pe.wait_ge(square3_done, g + 1)
                    pe.matmul(psum[:, X0, 0:T], ones_mean[:, :], square3[:, :], start=True, stop=True).then_inc(var3_done, 1)

                def router(g):
                    pe.wait_ge(ffn_x_done, g + 1)
                    for t in range(4):
                        mm = pe.matmul(psum[0:QT, X0, 8 * t:8 * t + 8], ffn_x[:, t * QT:t * QT + QT], wg_sb[:, :], start=True, stop=True)
                    mm.then_inc(router_done, 1)

                def spread(g):
                    pe.wait_ge(diag_done, g + 1)
                    pe.matmul(psum[:, X1, 0:T], ones[0:QT, :], weight_diag[:, 0:4, :], start=True, stop=True).then_inc(spread_done, 1)
                    pe.matmul(psum[:, X0, 0:T], ones[0:QT, :], weight_diag[:, 4:8, :], start=True, stop=True).then_inc(spread_done, 1)

                def slot(g, j, odd, now=True, last=True, older=True):
                    at1, at2 = before(g, j, 1), before(g, j, 2)
                    one, two_back = (now if j >= 1 else last), (now if j >= 2 else last)
                    if one:
                        scores(*at1)
                    if j == 3 and last:
                        centre_h(g - 1)
                    if now:
                        project(g, j)
                        if j < 2:
                            values(g, 2 * j)
                            values(g, 2 * j + 1)
                    if j == 2 and last:
                        project_out(g - 1)
                    if two_back:
                        weigh(*at2, odd if j >= 2 else 1 - odd)
                    if j == 3 and last:
                        variance3(g - 1)
                    if j == 0 and older:
                        router(g - 2)
                    if j == 1 and older:
                        spread(g - 2)
                    if one:
                        logits(*at1)

                pe.wait_ge(k_fill, 2)
                pe.wait_ge(v_fill, 4)
                pe.wait_ge(dve_fill, 2)
                pe.wait_ge(bank_left[ring("scores", PAIRS - 1)], 1)
                pe.wait_ge(attn_in, 32)
                for j in range(PAIRS):
                    slot(0, j, 0, last=False, older=False)
                for j in range(PAIRS):
                    slot(1, j, 1, older=False)
                with pe.Fori(2, GROUPS, 2) as g:
                    for odd in range(2):
                        for j in range(PAIRS):
                            slot(g + odd, j, odd)
                for j in range(PAIRS):
                    slot(GROUPS, j, 0, now=False)
                for j in range(2):
                    slot(GROUPS + 1, j, 1, now=False, last=False)

            @block.scalar
            def _(act):
                def high(g, j):
                    n = PAIRS * g + j
                    act.wait_ge(rope_done, 2 * n + 1)
                    if not (known(g) and g == 0):
                        act.wait_ge(logits_done, n - PAIRS + 1)
                    nc.scalar.activation(q_hi[:, j, :], q_sum[:, j % 2, :], ACT.Copy).then_inc(qk_hi_done, 1)
                    act.wait_ge(rope_done, 2 * n + 2)
                    for h in range(2):
                        rows = slice(TAB * h, TAB * h + TAB)
                        nc.scalar.activation(k_hi[rows, j, :, TAB * h:TAB * h + N],
                                             k_sum[rows, j % 2, :].rearrange("p (b n) -> p b n", b=GI), ACT.Copy).then_inc(qk_hi_done, 1)

                def high_values(g, p, odd):
                    act.wait_ge(proj_done, proj_count(g, "v", p))
                    if not (known(g) and g < 2):
                        act.wait_ge(pv_done, PAIRS * (g - 1))
                    for b in range(2):
                        for h in range(2):
                            src = bank("v", p)[TAB * b:TAB * b + N, :].rearrange("p (j h d) -> p j h d", j=PAIRS, h=2)
                            nc.scalar.activation(v_hi[odd][TAB * h:TAB * h + N, 2 * p + b, :, HD * h:HD * h + HD],
                                                 src[:, :, h, :], ACT.Copy).then_inc(v_hi_done, 1)

                def exponent(g, j):
                    n = PAIRS * g + j
                    act.wait_ge(logits_done, n + 1)
                    if not (known(g) and n < 2):
                        act.wait_ge(prob_lo_done, n - 1)
                    nc.scalar.activation(prob[:, j % 2, :], psum[:, LG, 0:T], ACT.Exp, scale=HD ** -0.5).then_inc(prob_done, 1)
                    if not (known(g) and n < 2):
                        act.wait_ge(pv_done, n - 1)
                    nc.scalar.activation(prob_hi[:, j % 2, :], psum[:, LG, 0:T], ACT.Exp, scale=HD ** -0.5).then_inc(prob_done, 1)

                def inverse(g, j):
                    n = PAIRS * g + j
                    act.wait_ge(den_done, n + 1)
                    if not (known(g) and n == 0):
                        act.wait_ge(heads_done, n)
                    nc.scalar.activation(inv_den[:, :], psum[:, DEN, 0:T], ACT.Ln).then_inc(log_den_done, 1)
                    act.wait_ge(log_den_done, n + 1)
                    nc.scalar.activation(inv_den[:, :], inv_den[:, :], ACT.Exp, scale=-1.0).then_inc(inv_done, 1)

                def square_h(g):
                    act.wait_ge(centre_done, g + 1)
                    if not (known(g) and g == 0):
                        act.wait_ge(ffn_x_done, g)
                    nc.scalar.activation(square3[:, :], psum[:, X1, 0:T], ACT.Square).then_inc(square3_done, 1)

                def norm3(g):
                    act.wait_ge(var3_done, g + 1)
                    nc.scalar.activation(rstd3[:, :], psum[:, X0, 0:T], ACT.Ln, bias=eps_ln).then_inc(log3_done, 1)
                    act.wait_ge(log3_done, g + 1)
                    nc.scalar.activation(rstd3[:, :], rstd3[:, :], ACT.Exp, scale=-0.5).then_inc(rstd3_done, 1)

                def router_ratio(g):
                    act.wait_ge(small_done, 4 * g + 1)
                    nc.scalar.activation(ratio[:, :], gap[:, :], ACT.Exp).then_inc(ratio_done, 1)

                def keep_scales(g):
                    for i, x in enumerate((X1, X0)):
                        act.wait_ge(spread_done, 2 * g + i + 1)
                        nc.scalar.activation(scales[:, bass.ds(g, 1), i * T:i * T + T], psum[:, x, 0:T].unsqueeze(1), ACT.Copy).then_inc(scales_done, 1)

                def slot(g, j, odd, now=True, last=True, older=True):
                    at2 = before(g, j, 2)
                    two_back = now if j >= 2 else last
                    if two_back:
                        exponent(*at2)
                    if j == 3 and last:
                        square_h(g - 1)
                    if j == 0 and older:
                        norm3(g - 2)
                    if j == 2 and older:
                        keep_scales(g - 2)
                    if now:
                        high(g, j)
                        if j < 2:
                            high_values(g, 2 * j, odd)
                            high_values(g, 2 * j + 1, odd)
                    if two_back:
                        inverse(*at2)
                    if j == 0 and older:
                        router_ratio(g - 2)

                act.preload_act_table_set("natural_log_exp_and_others")
                act.wait_ge(k_fill, 2)
                act.wait_ge(v_fill, 4)
                for j in range(PAIRS):
                    slot(0, j, 0, last=False, older=False)
                for j in range(PAIRS):
                    slot(1, j, 1, older=False)
                with act.Fori(2, GROUPS, 2) as g:
                    for odd in range(2):
                        for j in range(PAIRS):
                            slot(g + odd, j, odd)
                for j in range(PAIRS):
                    slot(GROUPS, j, 0, now=False)
                for j in range(3):
                    slot(GROUPS + 1, j, 1, now=False, last=False)

            @block.vector
            def _(dve):
                def split(g):
                    if not (known(g) and g == 0):
                        dve.wait_ge(proj_done, len(PROJ) * g)
                    here = normed[:, bass.ds(g * T, T)]
                    nc.vector.tensor_copy(x_hi[:, 0:T], here).then_inc(x_hi_done, 1)
                    dve.wait_ge(x_hi_done, g + 1)
                    nc.vector.tensor_tensor(x_lo[:, 0:T], here, x_hi[:, 0:T].bitcast(F32), ALU.subtract).then_inc(x_lo_done, 1)
                    dve.wait_ge(x_lo_done, g + 1)
                    for to, part in ((xv_hi, x_hi), (xv_lo, x_lo)):
                        nc.vector.tensor_copy(to[:, :, 0:N], part[:, :].bitcast(F32).rearrange("p (b n) -> p b n", b=GI)).then_inc(xv_done, 1)

                def rope(g, j, side):
                    for n, table in ((2 * side, cos), (2 * side + 1, sin)):
                        dve.wait_ge(proj_done, proj_count(g, "qk", 4 * j + n))
                        if not (known(g) and g == 0 and j == 0):
                            dve.wait_ge(rope_done, 2 * (PAIRS * g + j) - 1 + side)
                        nc.vector.tensor_tensor(term[:, n, :], bank("qk", 4 * j + n)[:, 0:T], table,
                                                ALU.mult).then_inc(bank_left[ring("qk", 4 * j + n)], 1)

                def low_values(g, p, odd):
                    dve.wait_ge(v_hi_done, 16 * g + 4 * p + 4)
                    for b in range(2):
                        for h in range(2):
                            src = bank("v", p)[TAB * b:TAB * b + N, :].rearrange("p (j h d) -> p j h d", j=PAIRS, h=2)
                            where = (slice(TAB * h, TAB * h + N), 2 * p + b, slice(None), slice(HD * h, HD * h + HD))
                            done = nc.vector.tensor_tensor(v_lo[odd][where], src[:, :, h, :], v_hi[odd][where], ALU.subtract)
                            if b and h:
                                done.then_inc(bank_left[ring("v", p)], 1)

                def row_maximum(g, j):
                    n = PAIRS * g + j
                    dve.wait_ge(scores_done, n + 1)
                    if not (known(g) and n < 2):
                        dve.wait_ge(neg_done, n - 1)
                    nc.vector.tensor_reduce(row_max[:, j % 2, :], bank("scores", j)[:, 0:T].rearrange("p (b n) -> p b n", b=GI),
                                            AX_X, ALU.max).then_inc(bank_left[ring("scores", j)], 1)

                def low_prob(g, j):
                    n = PAIRS * g + j
                    dve.wait_ge(prob_done, 2 * n + 2)
                    if not (known(g) and n < 2):
                        dve.wait_ge(pv_done, n - 1)
                    nc.vector.tensor_tensor(prob_lo[:, j % 2, :], prob[:, j % 2, :], prob_hi[:, j % 2, :], ALU.subtract).then_inc(prob_lo_done, 1)

                def normalise(g, j):
                    n = PAIRS * g + j
                    dve.wait_ge(inv_done, n + 1)
                    dve.wait_ge(pv_done, n + 1)
                    if j == 0 and not (known(g) and g == 0):
                        dve.wait_ge(attn_done, g)
                    nc.vector.tensor_tensor(heads_out[:, j, :], psum[:, OUT, 0:T], inv_den[:, :], ALU.mult).then_inc(heads_done, 1)

                def add_residual(g):
                    dve.wait_ge(attn_done, g + 1)
                    here = residual[:, bass.ds(g * T, T)]
                    nc.vector.tensor_tensor(here, psum[:, X0, 0:T], here, ALU.add).then_inc(h1_done, 1)

                def norm_ffn(g):
                    dve.wait_ge(rstd3_done, g + 1)
                    nc.vector.tensor_tensor(ffn_x[:, :], psum[:, X1, 0:T], rstd3[:, :], ALU.mult).then_inc(ffn_x_done, 1)

                def router_top(g):
                    dve.wait_ge(router_done, g + 1)
                    nc.vector.tensor_copy(normed[:, bass.ds(g * T, T)], ffn_x[:, :]).then_inc(ffn_in_done, 1)
                    for t in range(4):
                        done = nc.vector.max(out=top[:, t, :], in_=psum[0:QT, X0, 8 * t:8 * t + 8])
                    done.then_inc(top_done, 1)
                    dve.wait_ge(top_done, g + 1)
                    nc.vector.tensor_tensor(gap[:, :], top[:, :, 1], top[:, :, 0], ALU.subtract).then_inc(small_done, 1)

                def router_weights(g):
                    dve.wait_ge(ratio_done, g + 1)
                    nc.vector.tensor_scalar(den2[:, :], ratio[:, :], 1.0, None, ALU.add).then_inc(small_done, 1)
                    dve.wait_ge(small_done, 4 * g + 2)
                    nc.vector.reciprocal(weight[:, 0, :], den2[:, :]).then_inc(small_done, 1)
                    dve.wait_ge(small_done, 4 * g + 3)
                    nc.vector.tensor_tensor(weight[:, 1, :], weight[:, 0, :], ratio[:, :], ALU.mult).then_inc(small_done, 1)
                    dve.wait_ge(small_done, 4 * g + 4)
                    nc.vector.tensor_tensor(weight_diag[:, :, :],
                                            weight[:, :, :].rearrange("p i t -> p (i t)").unsqueeze(2).broadcast_to([QT, 8, QT]),
                                            ident[0:QT, 0:QT].unsqueeze(1).broadcast_to([QT, 8, QT]), ALU.mult).then_inc(diag_done, 1)

                def slot(g, j, odd, now=True, last=True, older=True, split_next=True):
                    at1, at2 = before(g, j, 1), before(g, j, 2)
                    one, two_back = (now if j >= 1 else last), (now if j >= 2 else last)
                    if one:
                        row_maximum(*at1)
                    if now:
                        rope(g, j, 0)
                    if two_back:
                        low_prob(*at2)
                    if j == 0 and older:
                        norm_ffn(g - 2)
                    if j == 1 and older:
                        router_weights(g - 2)
                    if now:
                        rope(g, j, 1)
                    if j == 3 and split_next:
                        split(g + 1)
                    if now and j < 2:
                        low_values(g, 2 * j, odd)
                        low_values(g, 2 * j + 1, odd)
                    if j == 2 and last:
                        add_residual(g - 1)
                    if j == 0 and older:
                        router_top(g - 2)
                    if two_back:
                        normalise(*at2)

                nc.vector.memset(psum[:, RING:RING + 3, :], 0.0).then_inc(bank_left[ring("scores", PAIRS - 1)], 1)
                nc.vector.memset(xv_hi[:, :, :].bitcast(F32), 0.0).then_inc(dve_fill, 1)
                nc.vector.memset(xv_lo[:, :, :].bitcast(F32), 0.0).then_inc(dve_fill, 1)
                dve.wait_ge(dve_fill, 2)
                dve.wait_ge(bank_left[ring("scores", PAIRS - 1)], 1)
                split(0)
                for j in range(PAIRS):
                    slot(0, j, 0, last=False, older=False)
                for j in range(PAIRS):
                    slot(1, j, 1, older=False)
                with dve.Fori(2, GROUPS - 2, 2) as g:
                    for odd in range(2):
                        for j in range(PAIRS):
                            slot(g + odd, j, odd)
                for odd in range(2):
                    for j in range(PAIRS):
                        slot(GROUPS - 2 + odd, j, odd, split_next=not odd)
                for j in range(PAIRS):
                    slot(GROUPS, j, 0, now=False, split_next=False)
                for j in range(2):
                    slot(GROUPS + 1, j, 1, now=False, last=False, split_next=False)

            @block.gpsimd
            def _(pool):
                def rope_sum(g, j):
                    n = PAIRS * g + j
                    if not (known(g) and n < 2):
                        pool.wait_ge(qk_lo_done, 3 * (n - 2) + 3)
                    for k, to in enumerate((q_sum, k_sum)):
                        for i in (2 * k, 2 * k + 1):
                            pool.wait_ge(bank_left[ring("qk", 4 * j + i)], bank_turn(g, "qk", 4 * j + i) + 1)
                        nc.gpsimd.tensor_tensor(to[:, j % 2, :], term[:, 2 * k, :], term[:, 2 * k + 1, :], ALU.add).then_inc(rope_done, 1)

                def low(g, j):
                    n = PAIRS * g + j
                    pool.wait_ge(rope_done, 2 * n + 2)
                    pool.wait_ge(qk_hi_done, 3 * n + 1)
                    nc.gpsimd.tensor_tensor(q_lo[:, j, :], q_sum[:, j % 2, :], q_hi[:, j, :], ALU.subtract).then_inc(qk_lo_done, 1)
                    for h in range(2):
                        rows = slice(TAB * h, TAB * h + TAB)
                        pool.wait_ge(qk_hi_done, 3 * n + 2 + h)
                        if h:
                            pool.wait_ge(qk_lo_done, 3 * n + 2)
                        nc.gpsimd.tensor_tensor(k_lo[rows, j, :, TAB * h:TAB * h + N],
                                                k_sum[rows, j % 2, :].rearrange("p (b n) -> p b n", b=GI),
                                                k_hi[rows, j, :, TAB * h:TAB * h + N], ALU.subtract).then_inc(qk_lo_done, 1)
                    pool.wait_ge(qk_lo_done, 3 * n + 3)

                def negate(g, j):
                    n = PAIRS * g + j
                    pool.wait_ge(bank_left[ring("scores", j)], score_turn(g, j) + 1)
                    if not (known(g) and n < 2):
                        pool.wait_ge(logits_done, n - 1)
                    nc.gpsimd.tensor_tensor(neg_max[:, j % 2, :].rearrange("p (b n) -> p b n", b=GI),
                                            row_max[:, j % 2, :].unsqueeze(2).broadcast_to([128, GI, N]), neg_id, ALU.mult).then_inc(neg_done, 1)

                def slot(g, j, now=True, last=True):
                    if now if j >= 1 else last:
                        negate(*before(g, j, 1))
                    if now:
                        rope_sum(g, j)
                        low(g, j)

                for t in (k_hi, k_lo):
                    nc.gpsimd.memset(t[:, :, :, :].bitcast(F32), 0.0).then_inc(k_fill, 1)
                for t in (*v_hi, *v_lo):
                    nc.gpsimd.memset(t[:, :, :, :].bitcast(F32), 0.0).then_inc(v_fill, 1)
                pool.wait_ge(k_fill, 2)
                pool.wait_ge(v_fill, 4)
                for j in range(PAIRS):
                    slot(0, j, last=False)
                for j in range(PAIRS):
                    slot(1, j)
                with pool.Fori(2, GROUPS, 2) as g:
                    for odd in range(2):
                        for j in range(PAIRS):
                            slot(g + odd, j)
                slot(GROUPS, 0, now=False)

        two.close()

        with ExitStack() as own:
            DEPTH = 4
            LEAD = 4
            f_hi = sb("f_hi", [128, TOKENS], F32R, own)
            f_lo = sb("f_lo", [128, TOKENS], F32R, own)
            w2_sb = sb("w2_sb", [128, FC, D], F32, own)
            scaled = sb("scaled", [128, DEPTH, 2 * T], F32, own)
            act_out = sb("act_out", [128, DEPTH, 2 * T], F32, own)
            hidden = sb("hidden", [128, DEPTH, T], F32, own)
            result = sb("result", [128, 2, T], F32, own)

            W2_PARTS = 8
            w2_in = [sem(f"w2_in{i}") for i in range(W2_PARTS)]
            f_hi_done = sem("f_hi_done")
            f_split = sem("f_split")
            up_done = sem("up_done")
            scaled_done = sem("scaled_done")
            gelu_done = sem("gelu_done")
            hidden_done = sem("hidden_done")
            down_done = sem("down_done")
            result_done = sem("result_done")
            stored = sem("stored")

            SUM = 7
            block = own.enter_context(nc.Block())

            @block.tensor
            def _(pe):
                def up(g, c):
                    n = FC * g + c
                    if c == 0:
                        pe.wait_ge(f_split, g + 1)
                    if not (isinstance(g, int) and n < DEPTH):
                        pe.wait_ge(scaled_done, n - DEPTH + 1)
                    xs = bass.ds(g * T, T)
                    to = psum[:, c % DEPTH, 0:T]
                    ws = slice(c * D, c * D + D)
                    pe.matmul(to, w1_hi[:, ws], f_hi[:, xs], start=True, stop=False)
                    pe.matmul(to, w1_hi[:, ws], f_lo[:, xs], start=False, stop=False)
                    pe.matmul(to, w1_lo[:, ws], f_hi[:, xs], start=False, stop=True).then_inc(up_done, 1)

                def down(g, c):
                    pe.wait_ge(hidden_done, FC * g + c + 1)
                    if isinstance(g, int) and g == 0 and c % (FC // W2_PARTS) == 0:
                        pe.wait_ge(w2_in[c // (FC // W2_PARTS)], 16)
                    if c == 0 and not (isinstance(g, int) and g == 0):
                        pe.wait_ge(result_done, g)
                    pe.matmul(psum[:, SUM, 0:T], w2_sb[:, c, :], hidden[:, c % DEPTH, :],
                              start=(c == 0), stop=(c == FC - 1)).then_inc(down_done, 1)

                for c in range(LEAD):
                    up(0, c)
                for c in range(LEAD, FC):
                    up(0, c)
                    down(0, c - LEAD)
                pe.wait_ge(w2_in[W2_PARTS - 1], 16)
                with pe.Fori(1, GROUPS) as g:
                    for c in range(FC):
                        up(g, c)
                        if c < LEAD:
                            down(g - 1, FC - LEAD + c)
                        else:
                            down(g, c - LEAD)
                for c in range(FC - LEAD, FC):
                    down(GROUPS - 1, c)

            @block.vector
            def _(dve):
                def split(g):
                    here = bass.ds(g * T, T)
                    nc.vector.tensor_copy(f_hi[:, here], normed[:, here]).then_inc(f_hi_done, 1)
                    dve.wait_ge(f_hi_done, g + 1)
                    nc.vector.tensor_tensor(f_lo[:, here], normed[:, here], f_hi[:, here].bitcast(F32), ALU.subtract).then_inc(f_split, 1)

                def scale(g, c):
                    n = FC * g + c
                    dve.wait_ge(up_done, n + 1)
                    if not (isinstance(g, int) and n < DEPTH):
                        dve.wait_ge(gelu_done, n - DEPTH + 1)
                    nc.vector.tensor_tensor(scaled[:, c % DEPTH, :].rearrange("p (i t) -> p i t", i=2),
                                            psum[:, c % DEPTH, 0:T].unsqueeze(1).broadcast_to([128, 2, T]),
                                            scales[:, bass.ds(g, 1), :].rearrange("p a (i t) -> p (a i) t", i=2),
                                            ALU.mult).then_inc(scaled_done, 1)

                def finish(g):
                    dve.wait_ge(down_done, FC * (g + 1))
                    if not (isinstance(g, int) and g == 0):
                        dve.wait_ge(stored, 16 * g)
                    nc.vector.scalar_tensor_tensor(out=result[:, 0, :], in0=psum[:, SUM, 0:T], scalar=b2_sum,
                                                   in1=residual[:, bass.ds(g * T, T)], op0=ALU.add, op1=ALU.add).then_inc(result_done, 1)

                split(0)
                for c in range(FC):
                    scale(0, c)
                    if c == FC // 2:
                        split(1)
                with dve.Fori(1, GROUPS - 1) as g:
                    for c in range(FC):
                        scale(g, c)
                        if c == LEAD:
                            finish(g - 1)
                        if c == FC // 2:
                            split(g + 1)
                last = GROUPS - 1
                for c in range(FC):
                    scale(last, c)
                    if c == LEAD:
                        finish(last - 1)
                finish(last)

            @block.scalar
            def _(act):
                def gelu(g, c):
                    n = FC * g + c
                    act.wait_ge(scaled_done, n + 1)
                    if not (isinstance(g, int) and n < DEPTH):
                        act.wait_ge(hidden_done, n - DEPTH + 1)
                    nc.scalar.activation(act_out[:, c % DEPTH, :], scaled[:, c % DEPTH, :], ACT.Gelu,
                                         bias=vec[:, V_B1 + c:V_B1 + c + 1]).then_inc(gelu_done, 1)

                act.preload_act_table(ACT.Gelu)
                for c in range(FC):
                    gelu(0, c)
                with act.Fori(1, GROUPS) as g:
                    for c in range(FC):
                        gelu(g, c)

            @block.gpsimd
            def _(pool):
                def add(g, c):
                    n = FC * g + c
                    pool.wait_ge(gelu_done, n + 1)
                    if not (isinstance(g, int) and n < DEPTH):
                        pool.wait_ge(down_done, n - DEPTH + 1)
                    nc.gpsimd.tensor_tensor(hidden[:, c % DEPTH, :], act_out[:, c % DEPTH, 0:T], act_out[:, c % DEPTH, T:2 * T],
                                            ALU.add).then_inc(hidden_done, 1)

                for c in range(FC):
                    add(0, c)
                with pool.Fori(1, GROUPS) as g:
                    for c in range(FC):
                        add(g, c)

            @block.sync
            def _(sp):
                for i in range(W2_PARTS):
                    part = slice(i * FC // W2_PARTS, (i + 1) * FC // W2_PARTS)
                    sp.dma_start(w2_sb[:, part, :], w2[:, part, :]).then_inc(w2_in[i], 16)
                with sp.Fori(0, GROUPS) as g:
                    sp.wait_ge(result_done, g + 1)
                    sp.dma_start(out[:, bass.ds(g * T, T)], result[:, 0, :]).then_inc(stored, 16)
                sp.wait_ge(stored, 16 * GROUPS)


def _constants():
    c = np.zeros((128, C_WIDTH), np.float32)
    c[:, C_IDENT:C_IDENT + 128] = np.eye(128)
    c[:, C_CENTRE:C_CENTRE + 128] = np.eye(128) - 1.0 / D
    p = np.arange(128)
    same = (p[:, None] // TAB) == (p[None, :] // TAB)
    real = (p % TAB) < N
    c[:, C_HEADS:C_HEADS + 128] = same & real[None, :] & real[:, None]
    c[:, C_HEADROWS:C_HEADROWS + 128] = same & real[:, None]
    c[:, C_NEGID:C_NEGID + N] = -1.0 * ((p[:, None] % TAB) == np.arange(N)[None, :])
    inv_freq = (1.0 / np.float32(10000.0) ** (np.arange(0, HD, 2, dtype=np.float32) / np.float32(HD))).astype(np.float32)
    angle = (inv_freq[(p % HD) // 2][:, None] * np.arange(N, dtype=np.float32)[None, :]).astype(np.float32)
    sign = np.where(p % 2 == 0, -1.0, 1.0)[:, None]
    c[:, C_COS:C_COS + T] = np.tile(np.cos(angle), (1, GI))
    c[:, C_SIN:C_SIN + T] = np.tile(sign * np.sin(angle), (1, GI))
    return c


def _patch_order():
    return [(a, b) for a in range(-1, PATCH + 1) for b in range(-1, PATCH + 1)
            if not (a in (-1, PATCH) and b in (-1, PATCH))]


def _layout_patches(x):
    side = SIDE * PATCH
    padded = np.zeros((IMAGES, side + 2, side + 2, CH), x.dtype)
    padded[:, 1:-1, 1:-1] = x
    order = np.array(_patch_order()) + 1
    starts = PATCH * np.arange(SIDE)[:, None]
    rows, columns = starts + order[:, 0], starts + order[:, 1]
    taken = padded[:, rows[:, None, :], columns[None, :, :], :]
    taken = taken.reshape(GROUPS, T, KC, KP)
    return np.ascontiguousarray(taken.transpose(0, 3, 2, 1))


def _layout_conv(w):
    out = np.zeros((5, PATCH + 2, PATCH + 2, CH, D), w.dtype)
    w = w.reshape(PATCH, PATCH, 5, CH, D)
    for s, (dy, dx) in enumerate(((0, 0), (0, -1), (0, 1), (-1, 0), (1, 0))):
        out[s, 1 + dy:1 + dy + PATCH, 1 + dx:1 + dx + PATCH] = w[:, :, s]
    order = np.array(_patch_order()) + 1
    out = out[:, order[:, 0], order[:, 1]].reshape(5, PARTS, PC, KP, D)
    return np.ascontiguousarray(out.transpose(3, 1, 0, 2, 4).reshape(KP, PARTS, 5, PC * D))


def kernel(x, L0_tok_conv_w, L0_tok_conv_b, L0_tok_gamma, L0_tok_beta, L0_tok_dense_w, L0_tok_dense_b,
           L0_attn_gamma, L0_attn_w_qkv, L0_attn_w_out, L0_ffn_Wg, L0_ffn_W1, L0_ffn_b1, L0_ffn_W2, L0_ffn_b2):
    import concourse.bacc as bacc
    from concourse.bass_utils import run_bass_kernel_spmd

    def arr(a):
        return np.asarray(a)

    vectors = np.zeros((128, V_WIDTH), np.float32)
    for col, v in ((V_CONVB, L0_tok_conv_b), (V_GAMMA, L0_tok_gamma), (V_BETA, L0_tok_beta),
                   (V_DENSEB, L0_tok_dense_b), (V_ATTNG, L0_attn_gamma)):
        vectors[:, col] = arr(v)
    vectors[:, V_B1:V_B1 + FC] = arr(L0_ffn_b1).reshape(FC, D).T
    vectors[:, V_B2:V_B2 + EXPERTS] = arr(L0_ffn_b2).T
    arrays = {
        "patches": _layout_patches(arr(x)),
        "shifted_w": _layout_conv(arr(L0_tok_conv_w)),
        "vectors": vectors,
        "dense_w": arr(L0_tok_dense_w),
        "w_qkv": arr(L0_attn_w_qkv),
        "w_out": arr(L0_attn_w_out).reshape(PAIRS, D, D).transpose(1, 0, 2),
        "w_gate": arr(L0_ffn_Wg),
        "w1": arr(L0_ffn_W1).transpose(1, 0, 2).reshape(D, EXPERTS * DFF),
        "w2": arr(L0_ffn_W2).reshape(FC, D, D).transpose(1, 0, 2),
        "consts": _constants(),
    }
    arrays = {k: np.ascontiguousarray(v) for k, v in arrays.items()}
    nc = bacc.Bacc("TRN2", target_bir_lowering=False, num_devices=1)
    ins = [nc.dram_tensor(f"in_{k}", v.shape, mybir.dt.from_np(v.dtype), kind="ExternalInput").ap() for k, v in arrays.items()]
    out = nc.dram_tensor("out_0", (D, TOKENS), F32, kind="ExternalOutput").ap()
    vit_tower(nc, *ins, out)
    r = run_bass_kernel_spmd(nc, [{f"in_{k}": v for k, v in arrays.items()}], core_ids=[0])
    got = r.results[0]["out_0"]
    return np.ascontiguousarray(got.T).reshape(IMAGES, N, D)
```

```python
from contextlib import ExitStack

import numpy as np

import concourse.bass as bass
from concourse import mybir

F32 = mybir.dt.float32
F32R = mybir.dt.float32r
F16 = mybir.dt.float16
ALU = mybir.AluOpType
ACT = mybir.ActivationFunctionType
AX_X = mybir.AxisListType.X

D = 128
N = 49
IMAGES = 64
GROUPS = 8
GI = IMAGES // GROUPS
T = GI * N
TOKENS = IMAGES * N
PATCH, SIDE, CH = 16, 7, 3
K_CONV = 960
KC = 8
KP = K_CONV // KC
PARTS = 4
PC = KC // PARTS
PAIRS = 4
HD = 64
QT = T // 4
EXPERTS, DFF = 8, 512
FC = EXPERTS * DFF // D
W1_PART = EXPERTS * DFF // GROUPS
TAB = 64
LOG_SCALE = 2.0 ** 20
RMS_FLOOR = (1e-8 ** 2 / D) * 1e-5

C_IDENT, C_CENTRE, C_HEADS, C_HEADROWS, C_NEGID, C_COS, C_SIN = 0, 128, 256, 384, 512, 561, 610
C_WIDTH = C_SIN + 49
V_CONVB, V_GAMMA, V_BETA, V_DENSEB, V_ATTNG, V_B1, V_B2 = 0, 1, 2, 3, 4, 5, 37
V_WIDTH = 45


def vit_tower(nc, patches, shifted_w, vectors, dense_w, w_qkv, w_out, w_gate, w1, w2, consts, out):
    with ExitStack() as ctx:
        def sem(name):
            return ctx.enter_context(nc.semaphore(name))

        def sb(name, shape, dt=F32, scope=ctx):
            return scope.enter_context(nc.sbuf_tensor(name, shape, dt))

        psum = ctx.enter_context(nc.psum_tensor("psum", [128, 8, 512], F32))
        const = sb("const", [128, C_WIDTH])
        vec = sb("vec", [128, V_WIDTH])
        ident = const[:, C_IDENT:C_IDENT + 128]
        centre = const[:, C_CENTRE:C_CENTRE + 128]
        ones = sb("ones", [128, 128])
        ones_mean = sb("ones_mean", [128, 128])
        cols = sb("cols", [128, 4])
        eps_conv, eps_ln, ln_shift, b2_sum = (cols[:, i:i + 1] for i in range(4))
        residual = sb("residual", [128, TOKENS])
        normed = sb("normed", [128, TOKENS])
        scales = sb("scales", [128, GROUPS, 2 * T])
        w1_hi = sb("w1_hi", [128, FC * D], F32R)
        w1_lo = sb("w1_lo", [128, FC * D], F32R)

        ratio = sb("ratio", [QT, 4])
        den2 = sb("den2", [QT, 4])
        weight = sb("weight", [QT, 2, 4])

        two = ctx.enter_context(ExitStack())
        wqk_hi = sb("wqk_hi", [128, 2, 8 * D], F32R, two)
        wqk_lo = sb("wqk_lo", [128, 2, 8 * D], F32R, two)
        wv_hi = sb("wv_hi", [128, 4 * D], F32R, two)
        wv_lo = sb("wv_lo", [128, 4 * D], F32R, two)
        wo_sb = sb("wo_sb", [128, PAIRS, D], F32, two)
        wg_sb = sb("wg_sb", [128, EXPERTS], F32, two)
        heads_r = sb("heads_r", [128, 128], F32R, two)
        headrows = sb("headrows", [128, 128], F16, two)

        k_hi = sb("k_hi", [128, PAIRS, GI, 2 * TAB], F16, two)
        k_lo = sb("k_lo", [128, PAIRS, GI, 2 * TAB], F16, two)
        v_hi = [sb(f"v_hi{i}", [128, GI, PAIRS, D], F16, two) for i in range(2)]
        v_lo = [sb(f"v_lo{i}", [128, GI, PAIRS, D], F16, two) for i in range(2)]

        x_hi = [sb("x_hi0", [128, GI, TAB], F32R, two)]
        x_lo = [sb("x_lo0", [128, GI, TAB], F32R, two)]

        with ExitStack() as own:
            shifts = sb("shifts", [KP, PARTS, 5, KC * D // PARTS], F32, own)
            conv_w = sb("conv_w", [KP, KC, D], F32, own)
            conv_mean = sb("conv_mean", [KP, KC], F32, own)
            patch = sb("patch", [KP, KC, T], F32, own)
            dense_raw = sb("dense_raw", [128, D], F32, own)
            dense_g = sb("dense_g", [128, D], F32, own)
            dense_c = sb("dense_c", [128, D], F32, own)
            dense_mean = sb("dense_mean", [128, 1], F32, own)
            conv_bc = sb("conv_bc", [128, 1], F32, own)
            dense_b = sb("dense_b", [128, 1], F32, own)
            dense_bc = sb("dense_bc", [128, 1], F32, own)
            raw = scales[:, :, :].rearrange("p g t -> p (g t)")
            w1_raw = raw[:, 0:FC * D]
            qkv_raw = raw[:, FC * D:FC * D + 12 * D]
            y = sb("y", [128, T], F32, own)
            square = sb("square", [128, T], F32, own)
            rstd1 = sb("rstd1", [128, T], F32, own)
            y_normed = sb("y_normed", [128, T], F32, own)
            square2 = sb("square2", [128, T], F32, own)
            floored = square2
            rstd2 = sb("rstd2", [128, T], F32, own)

            small_in = sem("small_in")
            shifts_in = [sem(f"shifts_in{c}") for c in range(PARTS)]
            qkv_in = sem("qkv_in")
            attn_in = sem("attn_in")
            ffn_in = sem("ffn_in")
            patch_in = [sem(f"patch_in{c}") for c in range(PARTS)]
            fills = sem("fills")
            fold = sem("fold")
            wprep = sem("wprep")
            conv_ready = sem("conv_ready")
            dense_ready = sem("dense_ready")
            bias_mm = sem("bias_mm")
            bias_ready = sem("bias_ready")
            kv_fill = sem("kv_fill")
            x_fill = sem("x_fill")
            x0_hi_done = sem("x0_hi_done")
            x0_lo_done = sem("x0_lo_done")
            qkv_steps = sem("qkv_steps")
            w1_hi_done = sem("w1_hi_done")
            qkv_hi_done = sem("qkv_hi_done")
            swap_done = sem("swap_done")
            conv_done = sem("conv_done")
            y_out = sem("y_out")
            var1_done = sem("var1_done")
            log1_done = sem("log1_done")
            rstd1_done = sem("rstd1_done")
            y_normed_done = sem("y_normed_done")
            dense_done = sem("dense_done")
            square2_done = sem("square2_done")
            residual_done = sem("residual_done")
            var2_done = sem("var2_done")
            floored_done = sem("floored_done")
            log2_done = sem("log2_done")
            rstd2_done = sem("rstd2_done")
            normed_done = sem("normed_done")

            Y, VAR1, PLAIN, CENTRED, VAR2, BIAS = (psum[:, i, 0:T] for i in range(6))

            block = own.enter_context(nc.Block())

            @block.sync
            def _(sp):
                for c in range(PARTS):
                    sp.dma_start(shifts[:, c, :, :], shifted_w[:, c, :, :]).then_inc(shifts_in[c], 16)

                def next_patches(g):
                    for c in range(PARTS):
                        sp.wait_ge(conv_done, (g - 1) * (PARTS) + c + 1)
                        sp.dma_start(patch[:, PC * c:PC * c + PC, :],
                                     patches[bass.ds(g, 1), :, PC * c:PC * c + PC, :].rearrange("a p c t -> p (a c) t")).then_inc(patch_in[c], 16)

                def load_w1(i):
                    here = bass.ds(i * W1_PART, W1_PART)
                    sp.dma_start(w1_raw[:, here], w1[:, here]).then_inc(ffn_in, 16)

                next_patches(1)
                load_w1(0)
                with sp.Fori(2, GROUPS) as g:
                    next_patches(g)
                    sp.wait_ge(w1_hi_done, g - 1)
                    load_w1(g - 1)
                sp.wait_ge(w1_hi_done, GROUPS - 1)
                load_w1(GROUPS - 1)

            @block.scalar
            def _(act):
                act.preload_act_table_set("natural_log_exp_and_others")
                for c in range(PARTS):
                    act.dma_start(patch[:, PC * c:PC * c + PC, :], patches[0, :, PC * c:PC * c + PC, :]).then_inc(patch_in[c], 16)
                act.dma_start(vec[:, :], vectors).then_inc(small_in, 16)
                act.dma_start(dense_raw[:, :], dense_w).then_inc(small_in, 16)
                act.dma_start(const[:, :], consts).then_inc(small_in, 16)
                act.dma_start(qkv_raw, w_qkv).then_inc(qkv_in, 16)
                act.dma_start(wo_sb[:, :, :], w_out).then_inc(attn_in, 16)
                act.dma_start(wg_sb[:, :], w_gate).then_inc(attn_in, 16)

                def leave_conv(g):
                    act.wait_ge(conv_done, (g + 1) * (PARTS))
                    if not (isinstance(g, int) and g == 0):
                        act.wait_ge(var1_done, g)
                    nc.scalar.activation(square[:, :], Y, ACT.Square, bias=conv_bc[:, 0:1]).then_inc(y_out, 1)
                    if not (isinstance(g, int) and g == 0):
                        act.wait_ge(y_normed_done, g)
                    nc.scalar.activation(y[:, :], Y, ACT.Identity, bias=conv_bc[:, 0:1]).then_inc(y_out, 1)

                def norm1(g):
                    act.wait_ge(var1_done, g + 1)
                    nc.scalar.activation(rstd1[:, :], VAR1, ACT.Ln, bias=eps_conv).then_inc(log1_done, 1)
                    act.wait_ge(log1_done, g + 1)
                    nc.scalar.activation(rstd1[:, :], rstd1[:, :], ACT.Exp, scale=-0.5).then_inc(rstd1_done, 1)

                def leave_dense(g):
                    act.wait_ge(dense_done, 2 * g + 1)
                    nc.scalar.activation(square2[:, :], CENTRED, ACT.Square, bias=dense_bc[:, 0:1]).then_inc(square2_done, 1)
                    act.wait_ge(dense_done, 2 * g + 2)
                    nc.scalar.activation(residual[:, bass.ds(g * T, T)], PLAIN, ACT.Identity, bias=dense_b[:, 0:1]).then_inc(residual_done, 1)

                def norm2(g):
                    act.wait_ge(floored_done, g + 1)
                    if not (isinstance(g, int) and g == 0):
                        act.wait_ge(normed_done, g)
                    nc.scalar.activation(rstd2[:, :], floored[:, :], ACT.Ln, scale=LOG_SCALE).then_inc(log2_done, 1)
                    act.wait_ge(log2_done, g + 1)
                    nc.scalar.activation(rstd2[:, :], rstd2[:, :], ACT.Exp, scale=-0.5, bias=ln_shift).then_inc(rstd2_done, 1)

                def split_w1(i):
                    act.wait_ge(ffn_in, 16 * i + 16)
                    here = bass.ds(i * W1_PART, W1_PART)
                    nc.scalar.activation(w1_hi[:, here], w1_raw[:, here], ACT.Copy).then_inc(w1_hi_done, 1)

                act.wait_ge(bias_ready, 1)
                leave_conv(0)
                norm1(0)
                act.wait_ge(qkv_steps, 1)
                nc.scalar.activation(wqk_hi[:, 0, :], qkv_raw[:, 0:8 * D], ACT.Copy).then_inc(qkv_hi_done, 1)
                nc.scalar.activation(wv_hi[:, :], qkv_raw[:, 8 * D:12 * D], ACT.Copy).then_inc(qkv_hi_done, 1)
                leave_conv(1)
                act.wait_ge(bias_ready, 3)
                leave_dense(0)
                split_w1(0)
                with act.Fori(2, GROUPS) as g:
                    norm2(g - 2)
                    norm1(g - 1)
                    split_w1(g - 1)
                    leave_conv(g)
                    leave_dense(g - 1)
                norm2(GROUPS - 2)
                norm1(GROUPS - 1)
                nc.scalar.activation(x_hi[0][:, :, 0:N], normed[:, 0:T].rearrange("p (b n) -> p b n", b=GI),
                                     ACT.Copy).then_inc(x0_hi_done, 1)
                split_w1(GROUPS - 1)
                leave_dense(GROUPS - 1)
                norm2(GROUPS - 1)

            @block.vector
            def _(dve):
                nc.vector.memset(ones[:, :], 1.0).then_inc(fills, 1)
                nc.vector.memset(ones_mean[:, :], 1.0 / D).then_inc(fills, 1)
                nc.vector.memset(eps_conv, 1e-3).then_inc(fills, 1)
                nc.vector.memset(eps_ln, 1e-5).then_inc(fills, 1)
                nc.vector.memset(ln_shift, 0.5 * float(np.log(LOG_SCALE))).then_inc(fills, 1)
                def prepare_dense():
                    dve.wait_ge(small_in, 48)
                    nc.vector.tensor_scalar(dense_g[:, :], dense_raw[:, :], vec[:, V_GAMMA:V_GAMMA + 1], None, ALU.mult).then_inc(wprep, 1)
                    dve.wait_ge(wprep, 1)
                    nc.vector.tensor_reduce(dense_mean[:, :], dense_g[:, :], AX_X, ALU.add).then_inc(wprep, 1)
                    dve.wait_ge(wprep, 2)
                    nc.vector.tensor_scalar(dense_mean[:, :], dense_mean[:, :], 1.0 / D, None, ALU.mult).then_inc(wprep, 1)
                    dve.wait_ge(wprep, 3)
                    nc.vector.tensor_scalar(dense_c[:, :], dense_g[:, :], dense_mean[:, 0:1], None, ALU.subtract).then_inc(dense_ready, 1)

                for c in range(PARTS):
                    here = conv_w[:, PC * c:PC * c + PC, :]
                    mean = conv_mean[:, PC * c:PC * c + PC]
                    shift = [shifts[:, c, k, :].rearrange("p (c d) -> p c d", c=PC) for k in range(5)]
                    at = 6 * c
                    dve.wait_ge(shifts_in[c], 16)
                    nc.vector.tensor_tensor(here, shift[0], shift[1], ALU.add).then_inc(fold, 1)
                    for k in range(2, 5):
                        dve.wait_ge(fold, at + k - 1)
                        nc.vector.tensor_tensor(here, here, shift[k], ALU.add).then_inc(fold, 1)
                    dve.wait_ge(fold, at + 4)
                    nc.vector.tensor_reduce(mean, here, AX_X, ALU.add).then_inc(fold, 1)
                    dve.wait_ge(fold, at + 5)
                    nc.vector.tensor_scalar(mean, mean, 1.0 / D, None, ALU.mult).then_inc(fold, 1)
                    dve.wait_ge(fold, at + 6)
                    nc.vector.tensor_tensor(here, here, mean.unsqueeze(2).broadcast_to([KP, PC, D]), ALU.subtract).then_inc(conv_ready, 1)
                dve.wait_ge(bias_mm, 1)
                nc.vector.tensor_copy(conv_bc[:, :], BIAS[:, 0:1]).then_inc(bias_ready, 1)
                prepare_dense()
                nc.vector.tensor_tensor(dense_b[:, :], BIAS[:, 1:2], vec[:, V_DENSEB:V_DENSEB + 1], ALU.add).then_inc(bias_ready, 1)
                dve.wait_ge(bias_mm, 2)
                nc.vector.tensor_copy(dense_bc[:, :], BIAS[:, 2:3]).then_inc(bias_ready, 1)
                nc.vector.tensor_copy(headrows[:, :], const[:, C_HEADROWS:C_HEADROWS + 128]).then_inc(wprep, 1)
                nc.vector.tensor_copy(heads_r[:, :], const[:, C_HEADS:C_HEADS + 128]).then_inc(wprep, 1)
                nc.vector.tensor_reduce(b2_sum, vec[:, V_B2:V_B2 + EXPERTS], AX_X, ALU.add).then_inc(wprep, 1)
                dve.wait_ge(wprep, 6)
                nc.vector.tensor_scalar(b2_sum, b2_sum, 2.0, None, ALU.mult).then_inc(wprep, 1)

                def scale1(g):
                    dve.wait_ge(rstd1_done, g + 1)
                    dve.wait_ge(y_out, 2 * g + 2)
                    if not (isinstance(g, int) and g == 0):
                        dve.wait_ge(dense_done, 2 * g)
                    nc.vector.tensor_tensor(y_normed[:, :], y[:, :], rstd1[:, :], ALU.mult).then_inc(y_normed_done, 1)

                def scale2(g):
                    dve.wait_ge(var2_done, g + 1)
                    if not (isinstance(g, int) and g == 0):
                        dve.wait_ge(log2_done, g)
                    nc.vector.tensor_scalar(floored[:, :], VAR2, RMS_FLOOR, None, ALU.max).then_inc(floored_done, 1)
                    dve.wait_ge(rstd2_done, g + 1)
                    nc.vector.scalar_tensor_tensor(out=normed[:, bass.ds(g * T, T)], in0=CENTRED, scalar=dense_bc[:, 0:1],
                                                   in1=rstd2[:, :], op0=ALU.add, op1=ALU.mult).then_inc(normed_done, 1)

                scale1(0)
                for part, src in enumerate((wqk_hi, wqk_lo)):
                    if part == 0:
                        dve.wait_ge(qkv_hi_done, 2)
                    else:
                        dve.wait_ge(qkv_steps, 3)
                    pairs = src[:, :, :].bitcast(F32).rearrange("p s (c e) -> p s c e", e=2)
                    outs = src[:, :, :].rearrange("p s (c e) -> p s c e", e=2)
                    nc.vector.tensor_copy(outs[:, 1, :, 0], pairs[:, 0, :, 1]).then_inc(swap_done, 1)
                    nc.vector.tensor_copy(outs[:, 1, :, 1], pairs[:, 0, :, 0]).then_inc(swap_done, 1)
                with dve.Fori(1, GROUPS) as g:
                    scale2(g - 1)
                    scale1(g)
                dve.wait_ge(x0_hi_done, 1)
                nc.vector.tensor_tensor(x_lo[0][:, :, 0:N], normed[:, 0:T].rearrange("p (b n) -> p b n", b=GI),
                                        x_hi[0][:, :, 0:N].bitcast(F32), ALU.subtract).then_inc(x0_lo_done, 1)
                scale2(GROUPS - 1)

            @block.gpsimd
            def _(pool):
                for t in (k_hi, k_lo, *v_hi, *v_lo):
                    nc.gpsimd.memset(t[:, :, :, :].bitcast(F32), 0.0).then_inc(kv_fill, 1)
                for t in (*x_hi, *x_lo):
                    nc.gpsimd.memset(t[:, :, N:TAB].bitcast(F32), 0.0).then_inc(x_fill, 1)
                pool.wait_ge(qkv_in, 16)
                pool.wait_ge(small_in, 48)
                nc.gpsimd.tensor_scalar(qkv_raw, qkv_raw, vec[:, V_ATTNG:V_ATTNG + 1], None, ALU.mult).then_inc(qkv_steps, 1)
                pool.wait_ge(qkv_hi_done, 2)
                nc.gpsimd.tensor_tensor(wv_lo[:, :], qkv_raw[:, 8 * D:12 * D], wv_hi[:, :].bitcast(F32), ALU.subtract).then_inc(qkv_steps, 1)
                nc.gpsimd.tensor_tensor(wqk_lo[:, 0, :], qkv_raw[:, 0:8 * D], wqk_hi[:, 0, :].bitcast(F32), ALU.subtract).then_inc(qkv_steps, 1)
                with pool.Fori(0, GROUPS) as i:
                    pool.wait_ge(w1_hi_done, i + 1)
                    here = bass.ds(i * W1_PART, W1_PART)
                    nc.gpsimd.tensor_tensor(w1_lo[:, here], w1_raw[:, here], w1_hi[:, here].bitcast(F32), ALU.subtract).then_inc(qkv_steps, 1)

            @block.tensor
            def _(pe):
                def conv(g, first, last):
                    if first == 0 and not (isinstance(g, int) and g == 0):
                        pe.wait_ge(y_out, 2 * g)
                    for c in range(first, last):
                        if c % PC == 0:
                            pe.wait_ge(patch_in[c // PC], 16 * g + 16)
                            if isinstance(g, int) and g == 0:
                                pe.wait_ge(conv_ready, c // PC + 1)
                        mm = pe.matmul(Y, conv_w[:, c, :], patch[:, c, :], start=(c == 0), stop=(c == KC - 1))
                        if c % PC == PC - 1:
                            mm.then_inc(conv_done, 1)

                def variance1(g):
                    pe.wait_ge(y_out, 2 * g + 1)
                    if not (isinstance(g, int) and g == 0):
                        pe.wait_ge(log1_done, g)
                    pe.matmul(VAR1, ones_mean[:, :], square[:, :], start=True, stop=True).then_inc(var1_done, 1)

                def dense(g):
                    pe.wait_ge(y_normed_done, g + 1)
                    if not (isinstance(g, int) and g == 0):
                        pe.wait_ge(normed_done, g)
                    pe.matmul(CENTRED, dense_c[:, :], y_normed[:, :], start=True, stop=True).then_inc(dense_done, 1)
                    if not (isinstance(g, int) and g == 0):
                        pe.wait_ge(residual_done, g)
                    pe.matmul(PLAIN, dense_g[:, :], y_normed[:, :], start=True, stop=True).then_inc(dense_done, 1)

                def variance2(g):
                    pe.wait_ge(square2_done, g + 1)
                    if not (isinstance(g, int) and g == 0):
                        pe.wait_ge(floored_done, g)
                    pe.matmul(VAR2, ones_mean[:, :], square2[:, :], start=True, stop=True).then_inc(var2_done, 1)

                conv(0, 0, KC - PC)
                pe.wait_ge(small_in, 48)
                pe.matmul(BIAS[:, 0:1], centre, vec[:, V_CONVB:V_CONVB + 1], start=True, stop=True)
                pe.matmul(BIAS[:, 1:2], dense_raw[:, :], vec[:, V_BETA:V_BETA + 1], start=True, stop=True).then_inc(bias_mm, 1)
                conv(0, KC - PC, KC)
                pe.wait_ge(fills, 5)
                conv(1, 0, 3)
                pe.wait_ge(bias_ready, 2)
                pe.matmul(BIAS[:, 2:3], centre, dense_b[:, :], start=True, stop=True).then_inc(bias_mm, 1)
                pe.wait_ge(dense_ready, 1)
                variance1(0)
                conv(1, 3, KC)
                dense(0)
                with pe.Fori(2, GROUPS) as g:
                    conv(g, 0, 1)
                    variance2(g - 2)
                    conv(g, 1, 3)
                    variance1(g - 1)
                    conv(g, 3, KC)
                    dense(g - 1)
                variance2(GROUPS - 2)
                variance1(GROUPS - 1)
                dense(GROUPS - 1)
                variance2(GROUPS - 1)

        with ExitStack() as own:
            x_hi.append(sb("x_hi1", [128, GI, TAB], F32R, own))
            x_lo.append(sb("x_lo1", [128, GI, TAB], F32R, own))
            term = sb("term", [128, 4, T], F32, own)
            q_sum = sb("q_sum", [128, 2, T], F32, own)
            k_sum = sb("k_sum", [128, 2, T], F32, own)
            q_hi = sb("q_hi", [128, PAIRS, T], F16, own)
            q_lo = sb("q_lo", [128, PAIRS, T], F16, own)
            row_max = sb("row_max", [128, 2, GI], F32, own)
            neg_max = sb("neg_max", [128, 2, T], F32R, own)
            prob = sb("prob", [128, 2, T], F32, own)
            prob_hi = sb("prob_hi", [128, 2, T], F16, own)
            prob_lo = sb("prob_lo", [128, 2, T], F16, own)
            inv_den = sb("inv_den", [128, T], F32, own)
            heads_out = sb("heads_out", [128, PAIRS, T], F32, own)
            square3 = sb("square3", [128, T], F32, own)
            rstd3 = square3
            ffn_x = sb("ffn_x", [128, T], F32, own)
            top = sb("top", [QT, 4, 8], F32, own)
            gap = sb("gap", [QT, 4], F32, own)
            weight_diag = sb("weight_diag", [QT, 8, QT], F32, own)

            x_hi_done = sem("x_hi_done")
            x_lo_done = sem("x_lo_done")
            x1_fill = sem("x1_fill")
            proj_done = sem("proj_done")
            values_done = sem("values_done")
            term_done = [sem(f"term_done{i}") for i in range(4)]
            rope_done = sem("rope_done")
            qk_hi_done = sem("qk_hi_done")
            low_k_done = sem("low_k_done")
            low_q_done = sem("low_q_done")
            v_hi_done = sem("v_hi_done")
            v_lo_done = sem("v_lo_done")
            scores_done = sem("scores_done")
            max_done = sem("max_done")
            neg_done = sem("neg_done")
            logits_done = sem("logits_done")
            prob_done = sem("prob_done")
            prob_lo_done = sem("prob_lo_done")
            den_done = sem("den_done")
            pv_done = sem("pv_done")
            log_den_done = sem("log_den_done")
            inv_done = sem("inv_done")
            heads_done = sem("heads_done")
            attn_done = sem("attn_done")
            h1_done = sem("h1_done")
            centre_done = sem("centre_done")
            square3_done = sem("square3_done")
            var3_done = sem("var3_done")
            log3_done = sem("log3_done")
            rstd3_done = sem("rstd3_done")
            ffn_x_done = sem("ffn_x_done")
            router_done = sem("router_done")
            ffn_in_done = sem("ffn_in_done")
            top_done = sem("top_done")
            small_done = sem("small_done")
            ratio_done = sem("ratio_done")
            diag_done = sem("diag_done")
            spread_done = sem("spread_done")
            scales_done = sem("scales_done")

            RING, LG, OUT, DEN, X0, X1 = 0, 3, 4, 5, 6, 7
            cos = const[:, C_COS:C_COS + N].unsqueeze(1).broadcast_to([128, GI, N])
            sin = const[:, C_SIN:C_SIN + N].unsqueeze(1).broadcast_to([128, GI, N])
            neg_id = const[:, C_NEGID:C_NEGID + N].unsqueeze(1).broadcast_to([128, GI, N])
            WIDE = N + 1

            BANK_QK, BANK_SCORES, BANK_V = (RING, RING + 1), RING + 2, RING + 2
            K, Q = 0, 1
            V_ITEMS = GROUPS * GI // 2

            def images(tile, width=N):
                return tile[:, 0:GI * width].rearrange("p (b n) -> p b n", b=GI)

            def before(g, j, back):
                return (g, j - back) if j >= back else (g - 1, j - back + PAIRS)

            def v_item(g, j, odd):
                return (g, j + 1, odd) if j < 3 else (g + 1, 0, 1 - odd)

            def known(g):
                return isinstance(g, int)

            def exists(pair_or_group):
                g = pair_or_group[0] if isinstance(pair_or_group, tuple) else pair_or_group
                return not known(g) or 0 <= g < GROUPS

            LAST = GROUPS - 1

            def weights_sum(dve, g):
                dve.wait_ge(ratio_done, g + 1)
                nc.vector.tensor_scalar(den2[:, :], ratio[:, :], 1.0, None, ALU.add).then_inc(small_done, 1)

            def weights_first(dve, g):
                dve.wait_ge(small_done, 4 * g + 2)
                nc.vector.reciprocal(weight[:, 0, :], den2[:, :]).then_inc(small_done, 1)

            def weights_second(dve, g):
                dve.wait_ge(small_done, 4 * g + 3)
                nc.vector.tensor_tensor(weight[:, 1, :], weight[:, 0, :], ratio[:, :], ALU.mult).then_inc(small_done, 1)

            def weights_diag(dve, g, i, to):
                dve.wait_ge(small_done, 4 * g + 4)
                nc.vector.tensor_tensor(to[:, 4 * i:4 * i + 4, :], weight[:, i, :].unsqueeze(2).broadcast_to([QT, 4, QT]),
                                        ident[0:QT, 0:QT].unsqueeze(1).broadcast_to([QT, 4, QT]), ALU.mult).then_inc(diag_done, 1)

            def router_weights(dve, g, to):
                weights_sum(dve, g)
                weights_first(dve, g)
                weights_second(dve, g)
                weights_diag(dve, g, 0, to)
                weights_diag(dve, g, 1, to)

            def out_bank(g):
                return RING + 1 if known(g) and g == LAST else X0

            def spread_bank(g, i):
                if known(g) and g == LAST - 1:
                    return (RING, RING + 2)[i]
                return X0

            FIRST, PAST = 3, GROUPS - 1

            def all_slots(engine, slot, past):
                for g in range(FIRST):
                    for j in range(PAIRS):
                        slot(g, j, g % 2)
                with engine.Fori(FIRST, PAST - 1, 2) as g:
                    for later in range(2):
                        for j in range(PAIRS):
                            slot(g + later, j, (FIRST + later) % 2)
                for g in range(PAST, past):
                    for j in range(PAIRS):
                        slot(g, j, g % 2)

            block = own.enter_context(nc.Block())

            @block.tensor
            def _(pe):
                def project(g, j, odd, side):
                    n = PAIRS * g + j
                    if j == 0 and side == K and not (known(g) and g == 0):
                        pe.wait_ge(x_lo_done, g)
                    for swapped in range(2):
                        if side == Q:
                            pe.wait_ge(term_done[swapped], n + 1)
                        elif not (known(g) and n == 0):
                            pe.wait_ge(term_done[2 + swapped], n)
                        at = ((1 - side) * PAIRS + j) * D
                        hi, lo = wqk_hi[:, swapped, at:at + D], wqk_lo[:, swapped, at:at + D]
                        to = images(psum[:, BANK_QK[swapped], :], WIDE)
                        pe.matmul(to, hi, x_hi[odd][:, :, 0:WIDE], start=True, stop=False)
                        pe.matmul(to, hi, x_lo[odd][:, :, 0:WIDE], start=False, stop=False)
                        pe.matmul(to, lo, x_hi[odd][:, :, 0:WIDE], start=False, stop=True).then_inc(proj_done, 1)

                def values(g, p, odd):
                    if not (known(g) and g == 0):
                        pe.wait_ge(x_lo_done, g)
                    n = PAIRS * g + p
                    if known(g) and n < 3:
                        if n:
                            pe.wait_ge(v_lo_done, n)
                    else:
                        pe.wait_ge(max_done, n - 2)
                    hi = x_hi[odd][:, 2 * p:2 * p + 2, :].rearrange("p b n -> p (b n)")
                    lo = x_lo[odd][:, 2 * p:2 * p + 2, :].rearrange("p b n -> p (b n)")
                    to = psum[:, BANK_V, :]
                    pe.matmul(to, hi, wv_hi[:, :], start=True, stop=False)
                    pe.matmul(to, lo, wv_hi[:, :], start=False, stop=False)
                    pe.matmul(to, hi, wv_lo[:, :], start=False, stop=True).then_inc(values_done, 1)

                def scores(g, j):
                    n = PAIRS * g + j
                    pe.wait_ge(qk_hi_done, 3 * n + 3)
                    pe.wait_ge(v_lo_done, min(n + 3, V_ITEMS) if known(g) else n + 3)
                    pe.ldweights(headrows[:, :], tile_position=(0, 0))
                    to = psum[:, BANK_SCORES, :]
                    for b in range(GI):
                        for h in range(2):
                            rows = slice(TAB * h, TAB * h + TAB)
                            mm = pe.matmul(to[TAB * h:TAB * h + N, b * N:b * N + N],
                                           q_hi[rows, j, b * N:b * N + N],
                                           k_hi[rows, j, b, TAB * h:TAB * h + N], start=True, stop=True)
                    mm.then_inc(scores_done, 1)

                def logits(g, j):
                    n = PAIRS * g + j
                    pe.wait_ge(neg_done, n + 1)
                    pe.wait_ge(low_k_done, 2 * n + 2)
                    pe.wait_ge(low_q_done, n + 1)
                    if not (known(g) and n == 0):
                        pe.wait_ge(prob_done, 2 * n)
                    pe.matmul(psum[:, LG, 0:T], heads_r[:, :], neg_max[:, j % 2, :], start=True, stop=False)
                    for b in range(GI):
                        to = psum[:, LG, b * N:b * N + N]
                        qs = slice(b * N, b * N + N)
                        pe.matmul(to, k_hi[:, j, b, :], q_hi[:, j, qs], start=False, stop=False)
                        pe.matmul(to, k_hi[:, j, b, :], q_lo[:, j, qs], start=False, stop=False)
                        mm = pe.matmul(to, k_lo[:, j, b, :], q_hi[:, j, qs], start=False, stop=(b == GI - 1))
                    mm.then_inc(logits_done, 1)

                def weigh(g, j, odd):
                    n = PAIRS * g + j
                    pe.wait_ge(prob_lo_done, n + 1)
                    if not (known(g) and n == 0):
                        pe.wait_ge(log_den_done, n)
                    pe.matmul(psum[:, DEN, 0:T], headrows[:, :], prob_hi[:, j % 2, :], start=True, stop=False)
                    pe.matmul(psum[:, DEN, 0:T], headrows[:, :], prob_lo[:, j % 2, :], start=False, stop=True).then_inc(den_done, 1)
                    if j == 0:
                        pe.wait_ge(v_lo_done, GI // 2 * (g + 1))
                    if not (known(g) and n == 0):
                        pe.wait_ge(heads_done, n)
                    for b in range(GI):
                        to = psum[:, OUT, b * N:b * N + N]
                        ps = slice(b * N, b * N + N)
                        pe.matmul(to, v_hi[odd][:, b, j, :], prob_hi[:, j % 2, ps], start=True, stop=False)
                        pe.matmul(to, v_hi[odd][:, b, j, :], prob_lo[:, j % 2, ps], start=False, stop=False)
                        mm = pe.matmul(to, v_lo[odd][:, b, j, :], prob_hi[:, j % 2, ps], start=False, stop=True)
                    mm.then_inc(pv_done, 1)

                def project_out(g, j):
                    pe.wait_ge(heads_done, PAIRS * g + j + 1)
                    if j == 0 and not (known(g) and (g == 0 or g == LAST)):
                        pe.wait_ge(log3_done, g)
                    mm = pe.matmul(psum[:, out_bank(g), 0:T], wo_sb[:, j, :], heads_out[:, j, :], start=(j == 0), stop=(j == PAIRS - 1))
                    if j == PAIRS - 1:
                        mm.then_inc(attn_done, 1)

                def centre_h(g):
                    pe.wait_ge(h1_done, g + 1)
                    if not (known(g) and g == 0):
                        pe.wait_ge(top_done, g)
                    pe.matmul(psum[:, X1, 0:T], centre, residual[:, bass.ds(g * T, T)], start=True, stop=True).then_inc(centre_done, 1)

                def variance3(g):
                    pe.wait_ge(square3_done, g + 1)
                    if not (known(g) and g == 0):
                        pe.wait_ge(scales_done, min(2 * g, 2 * (LAST - 1)) if known(g) else 2 * g)
                    if known(g) and g == LAST:
                        pe.wait_ge(log3_done, g)
                    pe.matmul(psum[:, X0, 0:T], ones_mean[:, :], square3[:, :], start=True, stop=True).then_inc(var3_done, 1)

                def router(g):
                    pe.wait_ge(ffn_x_done, g + 1)
                    for t in range(4):
                        mm = pe.matmul(psum[0:QT, X1, 8 * t:8 * t + 8], ffn_x[:, t * QT:t * QT + QT], wg_sb[:, :], start=True, stop=True)
                    mm.then_inc(router_done, 1)

                def spread(g, i):
                    pe.wait_ge(diag_done, 2 * g + i + 1)
                    if i and not (known(g) and g >= LAST - 1):
                        pe.wait_ge(scales_done, 2 * g + 1)
                    elif not (known(g) and g >= LAST - 1):
                        pe.wait_ge(h1_done, g + 2)
                    pe.matmul(psum[:, spread_bank(g, i), 0:T], ones[0:QT, :], weight_diag[:, 4 * i:4 * i + 4, :], start=True, stop=True).then_inc(spread_done, 1)

                def slot(g, j, odd):
                    out_proj = j == 3 and exists(g - 1) and not (known(g) and g > LAST)
                    if exists(g):
                        project(g, j, odd, K)
                    if out_proj:
                        project_out(g - 1, 0)
                    if exists(g) and exists(v_item(g, j, odd)):
                        values(*v_item(g, j, odd))
                    if out_proj:
                        project_out(g - 1, 1)
                    if exists(before(g, j, 2)):
                        logits(*before(g, j, 2))
                    if out_proj:
                        project_out(g - 1, 2)
                    if exists(g):
                        project(g, j, odd, Q)
                    if j == 1 and exists(g - 3):
                        spread(g - 3, 1)
                    if exists(before(g, j, 3)):
                        weigh(*before(g, j, 3), odd if j >= 3 else 1 - odd)
                    if exists(before(g, j, 1)):
                        scores(*before(g, j, 1))
                    if out_proj:
                        project_out(g - 1, 3)
                    if j == 0 and exists(g - 2):
                        centre_h(g - 2)
                    if j == 0 and exists(g - 3):
                        spread(g - 3, 0)
                    if j == 1 and exists(g - 2):
                        variance3(g - 2)
                    if j == 2 and exists(g - 2):
                        router(g - 2)
                    if known(g) and g > LAST:
                        project_out(LAST, j)

                pe.wait_ge(attn_in, 32)
                values(0, 0, 0)
                pe.wait_ge(x1_fill, 2)
                all_slots(pe, slot, GROUPS + 1)
                centre_h(LAST)
                spread(LAST - 1, 0)
                spread(LAST - 1, 1)
                variance3(LAST)
                router(LAST)

            @block.scalar
            def _(act):
                def high_x(g, odd):
                    if not (known(g) and g < 2):
                        act.wait_ge(proj_done, 4 * PAIRS * (g - 1))
                        act.wait_ge(values_done, GI // 2 * (g - 1))
                    nc.scalar.activation(x_hi[odd][:, :, 0:N], normed[:, bass.ds(g * T, T)].rearrange("p (b n) -> p b n", b=GI),
                                         ACT.Copy).then_inc(x_hi_done, 1)

                def high_q(g, j):
                    act.wait_ge(rope_done, 2 * (PAIRS * g + j) + 2)
                    nc.scalar.activation(q_hi[:, j, :], q_sum[:, j % 2, :], ACT.Copy).then_inc(qk_hi_done, 1)

                def high_k(g, j):
                    n = PAIRS * g + j
                    act.wait_ge(rope_done, 2 * n + 1)
                    if not (known(g) and g == 0):
                        act.wait_ge(logits_done, n - PAIRS + 1)
                    for h in range(2):
                        rows = slice(TAB * h, TAB * h + TAB)
                        nc.scalar.activation(k_hi[rows, j, :, TAB * h:TAB * h + N],
                                             images(k_sum[rows, j % 2, :]), ACT.Copy).then_inc(qk_hi_done, 1)

                def high_values(g, p, odd):
                    act.wait_ge(values_done, GI // 2 * g + p + 1)
                    if not (known(g) and g < 2):
                        act.wait_ge(pv_done, PAIRS * (g - 1))
                    for b in range(2):
                        for h in range(2):
                            src = psum[TAB * b:TAB * b + N, BANK_V, :].rearrange("p (j h d) -> p j h d", j=PAIRS, h=2)
                            nc.scalar.activation(v_hi[odd][TAB * h:TAB * h + N, 2 * p + b, :, HD * h:HD * h + HD],
                                                 src[:, :, h, :], ACT.Copy).then_inc(v_hi_done, 1)

                def exponent(g, j):
                    n = PAIRS * g + j
                    act.wait_ge(logits_done, n + 1)
                    if not (known(g) and n < 2):
                        act.wait_ge(prob_lo_done, n - 1)
                    nc.scalar.activation(prob[:, j % 2, :], psum[:, LG, 0:T], ACT.Exp, scale=HD ** -0.5).then_inc(prob_done, 1)
                    if not (known(g) and n < 2):
                        act.wait_ge(pv_done, n - 1)
                    nc.scalar.activation(prob_hi[:, j % 2, :], psum[:, LG, 0:T], ACT.Exp, scale=HD ** -0.5).then_inc(prob_done, 1)

                def inverse(g, j):
                    n = PAIRS * g + j
                    act.wait_ge(den_done, n + 1)
                    if not (known(g) and n == 0):
                        act.wait_ge(heads_done, n)
                    nc.scalar.activation(inv_den[:, :], psum[:, DEN, 0:T], ACT.Ln).then_inc(log_den_done, 1)
                    act.wait_ge(log_den_done, n + 1)
                    nc.scalar.activation(inv_den[:, :], inv_den[:, :], ACT.Exp, scale=-1.0).then_inc(inv_done, 1)

                def square_h(g):
                    act.wait_ge(centre_done, g + 1)
                    if not (known(g) and g == 0):
                        act.wait_ge(ffn_x_done, g)
                    nc.scalar.activation(square3[:, :], psum[:, X1, 0:T], ACT.Square).then_inc(square3_done, 1)

                def norm3(g):
                    act.wait_ge(var3_done, g + 1)
                    nc.scalar.activation(rstd3[:, :], psum[:, X0, 0:T], ACT.Ln, bias=eps_ln).then_inc(log3_done, 1)
                    act.wait_ge(log3_done, g + 1)
                    nc.scalar.activation(rstd3[:, :], rstd3[:, :], ACT.Exp, scale=-0.5).then_inc(rstd3_done, 1)

                def router_ratio(g):
                    act.wait_ge(small_done, 4 * g + 1)
                    nc.scalar.activation(ratio[:, :], gap[:, :], ACT.Exp).then_inc(ratio_done, 1)

                def keep_input(g):
                    act.wait_ge(ffn_x_done, g + 1)
                    nc.scalar.activation(normed[:, bass.ds(g * T, T)], ffn_x[:, :], ACT.Copy).then_inc(ffn_in_done, 1)

                def keep_scales(g, i):
                    act.wait_ge(spread_done, 2 * g + i + 1)
                    nc.scalar.activation(scales[:, bass.ds(g, 1), i * T:i * T + T], psum[:, spread_bank(g, i), 0:T].unsqueeze(1), ACT.Copy).then_inc(scales_done, 1)

                def slot(g, j, odd):
                    if exists(before(g, j, 1)):
                        high_q(*before(g, j, 1))
                    if j == 1 and exists(g - 2):
                        square_h(g - 2)
                    if j == 1 and exists(g - 3):
                        keep_scales(g - 3, 0)
                    if j == 2 and exists(g - 2):
                        norm3(g - 2)
                    if exists(g) and exists(v_item(g, j, odd)):
                        high_values(*v_item(g, j, odd))
                    if exists(g):
                        high_k(g, j)
                    if exists(before(g, j, 2)):
                        exponent(*before(g, j, 2))
                    if j == 1 and exists(g - 3):
                        keep_scales(g - 3, 1)
                    if exists(before(g, j, 3)):
                        inverse(*before(g, j, 3))
                    if j == 0 and exists(g + 1):
                        high_x(g + 1, 1 - odd)
                    if j == 2 and exists(g - 2):
                        keep_input(g - 2)
                    if j == 3 and exists(g - 2):
                        router_ratio(g - 2)

                high_values(0, 0, 0)
                all_slots(act, slot, GROUPS + 1)
                square_h(LAST)
                keep_scales(LAST - 1, 0)
                keep_scales(LAST - 1, 1)
                norm3(LAST)
                keep_input(LAST)
                router_ratio(LAST)

            @block.vector
            def _(dve):
                def low_x(g, odd):
                    dve.wait_ge(x_hi_done, g)
                    if not (known(g) and g < 2):
                        dve.wait_ge(proj_done, 4 * PAIRS * (g - 1))
                        dve.wait_ge(values_done, GI // 2 * (g - 1))
                    nc.vector.tensor_tensor(x_lo[odd][:, :, 0:N], normed[:, bass.ds(g * T, T)].rearrange("p (b n) -> p b n", b=GI),
                                            x_hi[odd][:, :, 0:N].bitcast(F32), ALU.subtract).then_inc(x_lo_done, 1)

                def rope(g, j, side):
                    n = PAIRS * g + j
                    for i, table in ((2 * side, cos), (2 * side + 1, sin)):
                        dve.wait_ge(proj_done, 4 * n + i + 1)
                        if not (known(g) and n == 0):
                            dve.wait_ge(rope_done, 2 * n - 1 + side)
                        nc.vector.tensor_tensor(images(term[:, i, :]), images(psum[:, BANK_QK[i % 2], :], WIDE)[:, :, 0:N], table,
                                                ALU.mult).then_inc(term_done[i], 1)

                def low_values(g, p, odd):
                    dve.wait_ge(v_hi_done, 16 * g + 4 * p + 4)
                    for b in range(2):
                        for h in range(2):
                            src = psum[TAB * b:TAB * b + N, BANK_V, :].rearrange("p (j h d) -> p j h d", j=PAIRS, h=2)
                            where = (slice(TAB * h, TAB * h + N), 2 * p + b, slice(None), slice(HD * h, HD * h + HD))
                            done = nc.vector.tensor_tensor(v_lo[odd][where], src[:, :, h, :], v_hi[odd][where], ALU.subtract)
                    done.then_inc(v_lo_done, 1)

                def row_maximum(g, j):
                    n = PAIRS * g + j
                    dve.wait_ge(scores_done, n + 1)
                    if not (known(g) and n < 2):
                        dve.wait_ge(neg_done, n - 1)
                    nc.vector.tensor_reduce(row_max[:, j % 2, :], images(psum[:, BANK_SCORES, :]), AX_X, ALU.max).then_inc(max_done, 1)

                def low_prob(g, j):
                    n = PAIRS * g + j
                    dve.wait_ge(prob_done, 2 * n + 2)
                    if not (known(g) and n < 2):
                        dve.wait_ge(pv_done, n - 1)
                    nc.vector.tensor_tensor(prob_lo[:, j % 2, :], prob[:, j % 2, :], prob_hi[:, j % 2, :], ALU.subtract).then_inc(prob_lo_done, 1)

                def normalise(g, j):
                    n = PAIRS * g + j
                    dve.wait_ge(inv_done, n + 1)
                    dve.wait_ge(pv_done, n + 1)
                    if j == 0 and not (known(g) and g == 0):
                        dve.wait_ge(attn_done, g)
                    nc.vector.tensor_tensor(heads_out[:, j, :], psum[:, OUT, 0:T], inv_den[:, :], ALU.mult).then_inc(heads_done, 1)

                def add_residual(g):
                    dve.wait_ge(attn_done, g + 1)
                    here = residual[:, bass.ds(g * T, T)]
                    nc.vector.tensor_tensor(here, psum[:, out_bank(g), 0:T], here, ALU.add).then_inc(h1_done, 1)

                def norm_ffn(g):
                    dve.wait_ge(rstd3_done, g + 1)
                    if not (known(g) and g == 0):
                        dve.wait_ge(ffn_in_done, g)
                    nc.vector.tensor_tensor(ffn_x[:, :], psum[:, X1, 0:T], rstd3[:, :], ALU.mult).then_inc(ffn_x_done, 1)

                def router_top(g):
                    for t in range(4):
                        done = nc.vector.max(out=top[:, t, :], in_=psum[0:QT, X1, 8 * t:8 * t + 8])
                    done.then_inc(top_done, 1)
                    dve.wait_ge(top_done, g + 1)
                    nc.vector.tensor_tensor(gap[:, :], top[:, :, 1], top[:, :, 0], ALU.subtract).then_inc(small_done, 1)

                def slot(g, j, odd):
                    weigh_last = j == 0 and exists(g - 3)
                    if weigh_last:
                        weights_sum(dve, g - 3)
                    if exists(g):
                        rope(g, j, K)
                    if j == 1 and exists(g - 3):
                        weights_diag(dve, g - 3, 1, weight_diag)
                    if weigh_last:
                        weights_first(dve, g - 3)
                    if exists(before(g, j, 3)):
                        low_prob(*before(g, j, 3))
                    if weigh_last:
                        weights_second(dve, g - 3)
                    if j == 3 and exists(g - 2):
                        dve.wait_ge(router_done, g - 1)
                    if exists(g - 1):
                        normalise(g - 1, j)
                    if j == 0 and exists(g - 2):
                        add_residual(g - 2)
                    if weigh_last:
                        weights_diag(dve, g - 3, 0, weight_diag)
                    if j == 1 and exists(g + 1):
                        low_x(g + 1, 1 - odd)
                    if j == 2 and exists(g - 2):
                        norm_ffn(g - 2)
                    if j == 3 and exists(g - 2):
                        router_top(g - 2)
                    if exists(g) and exists(v_item(g, j, odd)):
                        low_values(*v_item(g, j, odd))
                    if exists(g):
                        rope(g, j, Q)
                    if exists(before(g, j, 1)):
                        row_maximum(*before(g, j, 1))

                for t in (x_hi[1], x_lo[1]):
                    nc.vector.memset(t[:, :, N:TAB].bitcast(F32), 0.0).then_inc(x1_fill, 1)
                low_values(0, 0, 0)
                all_slots(dve, slot, GROUPS + 1)
                add_residual(LAST)
                router_weights(dve, LAST - 1, weight_diag)
                norm_ffn(LAST)
                dve.wait_ge(router_done, LAST + 1)
                router_top(LAST)

            @block.gpsimd
            def _(pool):
                def rope_sum(g, j, side):
                    n = PAIRS * g + j
                    if not (known(g) and n < 2):
                        pool.wait_ge(low_k_done, 2 * (n - 1))
                        pool.wait_ge(low_q_done, n - 1)
                    pool.wait_ge(term_done[2 * side], n + 1)
                    pool.wait_ge(term_done[2 * side + 1], n + 1)
                    to = (k_sum, q_sum)[side]
                    nc.gpsimd.tensor_tensor(to[:, j % 2, :], term[:, 2 * side, :], term[:, 2 * side + 1, :], ALU.add).then_inc(rope_done, 1)

                def low_k(g, j):
                    n = PAIRS * g + j
                    for h in range(2):
                        rows = slice(TAB * h, TAB * h + TAB)
                        pool.wait_ge(qk_hi_done, 3 * n + 1 + h)
                        if h:
                            pool.wait_ge(low_k_done, 2 * n + 1)
                        nc.gpsimd.tensor_tensor(k_lo[rows, j, :, TAB * h:TAB * h + N], images(k_sum[rows, j % 2, :]),
                                                k_hi[rows, j, :, TAB * h:TAB * h + N], ALU.subtract).then_inc(low_k_done, 1)
                    pool.wait_ge(low_k_done, 2 * n + 2)

                def low_q(g, j):
                    n = PAIRS * g + j
                    pool.wait_ge(rope_done, 2 * n + 2)
                    pool.wait_ge(qk_hi_done, 3 * n + 3)
                    nc.gpsimd.tensor_tensor(q_lo[:, j, :], q_sum[:, j % 2, :], q_hi[:, j, :], ALU.subtract).then_inc(low_q_done, 1)

                def negate(g, j):
                    n = PAIRS * g + j
                    pool.wait_ge(max_done, n + 1)
                    if not (known(g) and n < 2):
                        pool.wait_ge(logits_done, n - 1)
                    nc.gpsimd.tensor_tensor(neg_max[:, j % 2, :].rearrange("p (b n) -> p b n", b=GI),
                                            row_max[:, j % 2, :].unsqueeze(2).broadcast_to([128, GI, N]), neg_id, ALU.mult).then_inc(neg_done, 1)

                def slot(g, j):
                    if exists(before(g, j, 2)):
                        negate(*before(g, j, 2))
                    if exists(before(g, j, 1)):
                        low_q(*before(g, j, 1))
                    if exists(g):
                        rope_sum(g, j, K)
                    if exists(before(g, j, 1)):
                        low_k(*before(g, j, 1))
                    if exists(g):
                        rope_sum(g, j, Q)

                for j in range(PAIRS):
                    slot(0, j)
                with pool.Fori(1, GROUPS) as g:
                    for j in range(PAIRS):
                        slot(g, j)
                slot(GROUPS, 0)
                slot(GROUPS, 1)

        two.close()

        with ExitStack() as own:
            DEPTH = 4
            HIDDEN = 8
            LEAD = 6
            SPLIT_EVERY = 4
            f_hi = sb("f_hi", [128, TOKENS], F32R, own)
            f_lo = sb("f_lo", [128, TOKENS], F32R, own)
            w2_sb = sb("w2_sb", [128, FC, D], F32, own)
            scaled = sb("scaled", [128, DEPTH, 2 * T], F32, own)
            act_out = sb("act_out", [128, DEPTH, 2 * T], F32, own)
            hidden = sb("hidden", [128, HIDDEN, T], F32, own)
            hidden_hi = sb("hidden_hi", [128, 2, T], F32R, own)
            hidden_lo = sb("hidden_lo", [128, 2, T], F32R, own)
            w2_hi = sb("w2_hi", [128, FC // SPLIT_EVERY, D], F32R, own)
            w2_lo = sb("w2_lo", [128, FC // SPLIT_EVERY, D], F32R, own)
            result = sb("result", [128, T], F32, own)
            last_diag = sb("last_diag", [QT, 8, QT], F32, own)

            W2_PARTS = 8
            w2_in = [sem(f"w2_in{i}") for i in range(W2_PARTS)]
            f_hi_done = sem("f_hi_done")
            f_split = sem("f_split")
            up_done = sem("up_done")
            scaled_done = sem("scaled_done")
            gelu_done = sem("gelu_done")
            hidden_done = sem("hidden_done")
            w2_hi_done = sem("w2_hi_done")
            w2_lo_done = sem("w2_lo_done")
            hidden_hi_done = sem("hidden_hi_done")
            hidden_lo_done = sem("hidden_lo_done")
            down_done = sem("down_done")
            result_done = sem("result_done")
            stored = sem("stored")

            SUM = (6, 7)
            SPREAD = (4, 5)
            SPREAD_AT = 24
            HIGH_LAG, LOW_LAG = 2, 4

            def in_parts(c):
                return c % SPLIT_EVERY == SPLIT_EVERY - 1

            def part_count(g, c):
                return FC // SPLIT_EVERY * g + c // SPLIT_EVERY

            block = own.enter_context(nc.Block())

            @block.tensor
            def _(pe):
                def up(g, c):
                    n = FC * g + c
                    if c == 0:
                        pe.wait_ge(f_split, g + 1)
                    if not (isinstance(g, int) and n < DEPTH):
                        pe.wait_ge(scaled_done, n - DEPTH + 1)
                    xs = bass.ds(g * T, T)
                    to = psum[:, c % DEPTH, 0:T]
                    ws = slice(c * D, c * D + D)
                    pe.matmul(to, w1_hi[:, ws], f_hi[:, xs], start=True, stop=False)
                    pe.matmul(to, w1_hi[:, ws], f_lo[:, xs], start=False, stop=False)
                    pe.matmul(to, w1_lo[:, ws], f_hi[:, xs], start=False, stop=True).then_inc(up_done, 1)

                def down(g, c, odd):
                    if c == 0 and not (isinstance(g, int) and g < 2):
                        pe.wait_ge(result_done, g - 1)
                    to = psum[:, SUM[odd], 0:T]
                    if in_parts(c):
                        part = part_count(g, c)
                        if isinstance(g, int) and g == 0:
                            pe.wait_ge(w2_lo_done, part + 1)
                        pe.wait_ge(hidden_lo_done, part + 1)
                        w = c // SPLIT_EVERY
                        pe.matmul(to, w2_hi[:, w, :], hidden_hi[:, w % 2, :], start=False, stop=False)
                        pe.matmul(to, w2_hi[:, w, :], hidden_lo[:, w % 2, :], start=False, stop=False)
                        pe.matmul(to, w2_lo[:, w, :], hidden_hi[:, w % 2, :], start=False, stop=(c == FC - 1)).then_inc(down_done, 1)
                        return
                    pe.wait_ge(hidden_done, FC * g + c + 1)
                    if isinstance(g, int) and g == 0 and c % (FC // W2_PARTS) == 0:
                        pe.wait_ge(w2_in[c // (FC // W2_PARTS)], 16)
                    pe.matmul(to, w2_sb[:, c, :], hidden[:, c % HIDDEN, :], start=(c == 0), stop=False).then_inc(down_done, 1)

                for c in range(LEAD):
                    up(0, c)
                for c in range(LEAD, FC):
                    if c == SPREAD_AT:
                        for i in range(2):
                            pe.wait_ge(diag_done, 2 * LAST + i + 1)
                            pe.matmul(psum[:, SPREAD[i], 0:T], ones[0:QT, :], last_diag[:, 4 * i:4 * i + 4, :],
                                      start=True, stop=True).then_inc(spread_done, 1)
                    up(0, c)
                    down(0, c - LEAD, 0)
                pe.wait_ge(w2_in[W2_PARTS - 1], 16)
                pe.wait_ge(w2_lo_done, FC // SPLIT_EVERY)

                def group(g, odd):
                    for c in range(FC):
                        up(g, c)
                        if c < LEAD:
                            down(g - 1, FC - LEAD + c, 1 - odd)
                        else:
                            down(g, c - LEAD, odd)

                with pe.Fori(1, GROUPS - 2, 2) as g:
                    group(g, 1)
                    group(g + 1, 0)
                group(GROUPS - 1, 1)
                for c in range(FC - LEAD, FC):
                    down(GROUPS - 1, c, 1)

            @block.vector
            def _(dve):
                def split(g):
                    here = bass.ds(g * T, T)
                    nc.vector.tensor_copy(f_hi[:, here], normed[:, here]).then_inc(f_hi_done, 1)
                    dve.wait_ge(f_hi_done, g + 1)
                    nc.vector.tensor_tensor(f_lo[:, here], normed[:, here], f_hi[:, here].bitcast(F32), ALU.subtract).then_inc(f_split, 1)

                def scale(g, c):
                    n = FC * g + c
                    if c == 0 and isinstance(g, int) and g == LAST:
                        dve.wait_ge(scales_done, 2 * GROUPS)
                    dve.wait_ge(up_done, n + 1)
                    if not (isinstance(g, int) and n < DEPTH):
                        dve.wait_ge(gelu_done, n - DEPTH + 1)
                    nc.vector.tensor_tensor(scaled[:, c % DEPTH, :].rearrange("p (i t) -> p i t", i=2),
                                            psum[:, c % DEPTH, 0:T].unsqueeze(1).broadcast_to([128, 2, T]),
                                            scales[:, bass.ds(g, 1), :].rearrange("p a (i t) -> p (a i) t", i=2),
                                            ALU.mult).then_inc(scaled_done, 1)

                def low_w2(w):
                    dve.wait_ge(w2_hi_done, w + 1)
                    c = SPLIT_EVERY * w + SPLIT_EVERY - 1
                    nc.vector.tensor_tensor(w2_lo[:, w, :], w2_sb[:, c, :], w2_hi[:, w, :].bitcast(F32), ALU.subtract).then_inc(w2_lo_done, 1)

                def low_hidden(g, c):
                    part = part_count(g, c)
                    dve.wait_ge(hidden_hi_done, part + 1)
                    if not (isinstance(g, int) and part < 2):
                        dve.wait_ge(down_done, FC * g + c - 2 * SPLIT_EVERY + 1)
                    at = c // SPLIT_EVERY % 2
                    nc.vector.tensor_tensor(hidden_lo[:, at, :], hidden[:, c % HIDDEN, :], hidden_hi[:, at, :].bitcast(F32), ALU.subtract).then_inc(hidden_lo_done, 1)

                def finish(g, odd):
                    dve.wait_ge(down_done, FC * (g + 1))
                    if not (isinstance(g, int) and g == 0):
                        dve.wait_ge(stored, 16 * g)
                    nc.vector.scalar_tensor_tensor(out=result[:, :], in0=psum[:, SUM[odd], 0:T], scalar=b2_sum,
                                                   in1=residual[:, bass.ds(g * T, T)], op0=ALU.add, op1=ALU.add).then_inc(result_done, 1)

                def chunk(g, c):
                    scale(g, c)
                    if isinstance(g, int) and g == 0 and c % SPLIT_EVERY == 2:
                        low_w2(c // SPLIT_EVERY)
                    at = c - LOW_LAG
                    if in_parts(at % FC) and not (isinstance(g, int) and g == 0 and at < 0):
                        low_hidden(g if at >= 0 else g - 1, at % FC)

                split(0)
                for c in range(FC):
                    if c == SPREAD_AT // 2:
                        router_weights(dve, LAST, last_diag)
                    chunk(0, c)
                    if c == FC // 2:
                        split(1)

                def group(g, odd, more=True):
                    for c in range(FC):
                        if c == LEAD + 1:
                            finish(g - 1, 1 - odd)
                        chunk(g, c)
                        if c == FC // 2 and more:
                            split(g + 1)

                with dve.Fori(1, GROUPS - 2, 2) as g:
                    group(g, 1)
                    group(g + 1, 0)
                group(GROUPS - 1, 1, more=False)
                low_hidden(GROUPS - 1, FC - 1)
                finish(GROUPS - 1, 1)

            @block.scalar
            def _(act):
                def gelu(g, c):
                    n = FC * g + c
                    act.wait_ge(scaled_done, n + 1)
                    if not (isinstance(g, int) and n < DEPTH):
                        act.wait_ge(hidden_done, n - DEPTH + 1)
                    nc.scalar.activation(act_out[:, c % DEPTH, :], scaled[:, c % DEPTH, :], ACT.Gelu,
                                         bias=vec[:, V_B1 + c:V_B1 + c + 1]).then_inc(gelu_done, 1)

                def high_w2(w):
                    c = SPLIT_EVERY * w + SPLIT_EVERY - 1
                    act.wait_ge(w2_in[c // (FC // W2_PARTS)], 16)
                    nc.scalar.activation(w2_hi[:, w, :], w2_sb[:, c, :], ACT.Copy).then_inc(w2_hi_done, 1)

                def high_hidden(g, c):
                    part = part_count(g, c)
                    act.wait_ge(hidden_done, FC * g + c + 1)
                    if not (isinstance(g, int) and part < 2):
                        act.wait_ge(down_done, FC * g + c - 2 * SPLIT_EVERY + 1)
                    nc.scalar.activation(hidden_hi[:, c // SPLIT_EVERY % 2, :], hidden[:, c % HIDDEN, :], ACT.Copy).then_inc(hidden_hi_done, 1)

                def chunk(g, c):
                    gelu(g, c)
                    if isinstance(g, int) and g == 0 and c % SPLIT_EVERY == 0:
                        high_w2(c // SPLIT_EVERY)
                    at = c - HIGH_LAG
                    if in_parts(at % FC) and not (isinstance(g, int) and g == 0 and at < 0):
                        high_hidden(g if at >= 0 else g - 1, at % FC)

                act.preload_act_table(ACT.Gelu)
                for c in range(FC):
                    chunk(0, c)
                    if c in (SPREAD_AT, SPREAD_AT + 1):
                        i = c - SPREAD_AT
                        act.wait_ge(spread_done, 2 * LAST + i + 1)
                        nc.scalar.activation(scales[:, LAST, i * T:i * T + T], psum[:, SPREAD[i], 0:T], ACT.Copy).then_inc(scales_done, 1)
                with act.Fori(1, GROUPS) as g:
                    for c in range(FC):
                        chunk(g, c)
                high_hidden(GROUPS - 1, FC - 1)

            @block.gpsimd
            def _(pool):
                def add(g, c):
                    n = FC * g + c
                    pool.wait_ge(gelu_done, n + 1)
                    if not (isinstance(g, int) and n < HIDDEN):
                        pool.wait_ge(down_done, n - HIDDEN + 1)
                    nc.gpsimd.tensor_tensor(hidden[:, c % HIDDEN, :], act_out[:, c % DEPTH, 0:T], act_out[:, c % DEPTH, T:2 * T],
                                            ALU.add).then_inc(hidden_done, 1)

                for c in range(FC):
                    add(0, c)
                with pool.Fori(1, GROUPS) as g:
                    for c in range(FC):
                        add(g, c)

            @block.sync
            def _(sp):
                for i in range(W2_PARTS):
                    part = slice(i * FC // W2_PARTS, (i + 1) * FC // W2_PARTS)
                    sp.dma_start(w2_sb[:, part, :], w2[:, part, :]).then_inc(w2_in[i], 16)
                with sp.Fori(0, GROUPS) as g:
                    sp.wait_ge(result_done, g + 1)
                    sp.dma_start(out[:, bass.ds(g * T, T)], result[:, :]).then_inc(stored, 16)
                sp.wait_ge(stored, 16 * GROUPS)


def _constants():
    c = np.zeros((128, C_WIDTH), np.float32)
    c[:, C_IDENT:C_IDENT + 128] = np.eye(128)
    c[:, C_CENTRE:C_CENTRE + 128] = np.eye(128) - 1.0 / D
    p = np.arange(128)
    same = (p[:, None] // TAB) == (p[None, :] // TAB)
    real = (p % TAB) < N
    c[:, C_HEADS:C_HEADS + 128] = same & real[None, :] & real[:, None]
    c[:, C_HEADROWS:C_HEADROWS + 128] = same & real[:, None]
    c[:, C_NEGID:C_NEGID + N] = -1.0 * ((p[:, None] % TAB) == np.arange(N)[None, :])
    inv_freq = (1.0 / np.float32(10000.0) ** (np.arange(0, HD, 2, dtype=np.float32) / np.float32(HD))).astype(np.float32)
    angle = (inv_freq[(p % HD) // 2][:, None] * np.arange(N, dtype=np.float32)[None, :]).astype(np.float32)
    sign = np.where(p % 2 == 0, -1.0, 1.0)[:, None]
    c[:, C_COS:C_COS + N] = np.cos(angle)
    c[:, C_SIN:C_SIN + N] = sign * np.sin(angle)
    return c


def _patch_order():
    return [(a, b) for a in range(-1, PATCH + 1) for b in range(-1, PATCH + 1)
            if not (a in (-1, PATCH) and b in (-1, PATCH))]


def _layout_patches(x):
    side = SIDE * PATCH
    padded = np.zeros((IMAGES, side + 2, side + 2, CH), x.dtype)
    padded[:, 1:-1, 1:-1] = x
    order = np.array(_patch_order()) + 1
    starts = PATCH * np.arange(SIDE)[:, None]
    rows, columns = starts + order[:, 0], starts + order[:, 1]
    taken = padded[:, rows[:, None, :], columns[None, :, :], :]
    taken = taken.reshape(GROUPS, T, KC, KP)
    return np.ascontiguousarray(taken.transpose(0, 3, 2, 1))


def _layout_conv(w):
    out = np.zeros((5, PATCH + 2, PATCH + 2, CH, D), w.dtype)
    w = w.reshape(PATCH, PATCH, 5, CH, D)
    for s, (dy, dx) in enumerate(((0, 0), (0, -1), (0, 1), (-1, 0), (1, 0))):
        out[s, 1 + dy:1 + dy + PATCH, 1 + dx:1 + dx + PATCH] = w[:, :, s]
    order = np.array(_patch_order()) + 1
    out = out[:, order[:, 0], order[:, 1]].reshape(5, PARTS, PC, KP, D)
    return np.ascontiguousarray(out.transpose(3, 1, 0, 2, 4).reshape(KP, PARTS, 5, PC * D))


def kernel(x, L0_tok_conv_w, L0_tok_conv_b, L0_tok_gamma, L0_tok_beta, L0_tok_dense_w, L0_tok_dense_b,
           L0_attn_gamma, L0_attn_w_qkv, L0_attn_w_out, L0_ffn_Wg, L0_ffn_W1, L0_ffn_b1, L0_ffn_W2, L0_ffn_b2):
    import concourse.bacc as bacc
    from concourse.bass_utils import run_bass_kernel_spmd

    def arr(a):
        return np.asarray(a)

    vectors = np.zeros((128, V_WIDTH), np.float32)
    for col, v in ((V_CONVB, L0_tok_conv_b), (V_GAMMA, L0_tok_gamma), (V_BETA, L0_tok_beta),
                   (V_DENSEB, L0_tok_dense_b), (V_ATTNG, L0_attn_gamma)):
        vectors[:, col] = arr(v)
    vectors[:, V_B1:V_B1 + FC] = arr(L0_ffn_b1).reshape(FC, D).T
    vectors[:, V_B2:V_B2 + EXPERTS] = arr(L0_ffn_b2).T
    arrays = {
        "patches": _layout_patches(arr(x)),
        "shifted_w": _layout_conv(arr(L0_tok_conv_w)),
        "vectors": vectors,
        "dense_w": arr(L0_tok_dense_w),
        "w_qkv": arr(L0_attn_w_qkv),
        "w_out": arr(L0_attn_w_out).reshape(PAIRS, D, D).transpose(1, 0, 2),
        "w_gate": arr(L0_ffn_Wg),
        "w1": arr(L0_ffn_W1).transpose(1, 0, 2).reshape(D, EXPERTS * DFF),
        "w2": arr(L0_ffn_W2).reshape(FC, D, D).transpose(1, 0, 2),
        "consts": _constants(),
    }
    arrays = {k: np.ascontiguousarray(v) for k, v in arrays.items()}
    nc = bacc.Bacc("TRN2", target_bir_lowering=False, num_devices=1)
    ins = [nc.dram_tensor(f"in_{k}", v.shape, mybir.dt.from_np(v.dtype), kind="ExternalInput").ap() for k, v in arrays.items()]
    out = nc.dram_tensor("out_0", (D, TOKENS), F32, kind="ExternalOutput").ap()
    vit_tower(nc, *ins, out)
    r = run_bass_kernel_spmd(nc, [{f"in_{k}": v for k, v in arrays.items()}], core_ids=[0])
    got = r.results[0]["out_0"]
    return np.ascontiguousarray(got.T).reshape(IMAGES, N, D)
```
